# Optimizing a Trainium2 kernel written in Bass

```python
import numpy as np
import jax
import jax.numpy as jnp

def _softmax(x, axis=-1):
    return jax.nn.softmax(x, axis=axis)

def _gelu(x):
    return jax.nn.gelu(x, approximate=True)

def _silu(x):
    return jax.nn.silu(x)

def _sigmoid(x):
    return jax.nn.sigmoid(x)

def _layernorm(x, axis=-1, eps=1e-05):
    m = jnp.mean(x, axis=axis, keepdims=True)
    v = jnp.var(x, axis=axis, keepdims=True)
    return (x - m) / jnp.sqrt(v + eps)

def _scatter_add(tgt, idx, src, axis=0):
    return tgt.at[idx].add(src)

def _segment_sum(src, seg, n):
    return jax.ops.segment_sum(src, seg, n)
kernel_name = 'mk_flamingo_gated_d1_seqx_r4_1efb4c'

def setup_inputs(seed: int=0):
    np.random.seed(seed)
    _w = jnp.asarray

    def _rec_inputs():
        import jax
        import jax.numpy as jnp
        _rk = jax.random.key(seed)
        x = 7.22e-05 + 1 * jax.random.normal(jax.random.fold_in(_rk, 1), (8, 256, 512), jnp.float32)
        _lenS = 256 - jax.random.randint(jax.random.fold_in(_rk, 7), (8,), 0, max(1, 256 // 4) + 1, jnp.int32)
        _lenS2 = 256 - jax.random.randint(jax.random.fold_in(_rk, 8), (8,), 0, max(1, 256 // 4) + 1, jnp.int32)
        _ctx_512P = jax.random.normal(jax.random.fold_in(_rk, 11), (8, 16, 128), jnp.float32)
        _ctx_512c = jax.random.dirichlet(jax.random.fold_in(_rk, 511), 0.3 * jnp.ones((16,), jnp.float32), (8, 256))
        _ctx_512t = jnp.einsum('bsk,bkd->bsd', _ctx_512c, _ctx_512P)
        _ctx_512t = _ctx_512t * jax.lax.rsqrt(jnp.mean(jnp.square(_ctx_512t)) + 1e-12) * 0.953939
        ctx_512 = -0.000514642 + 1.00011 * (_ctx_512t + 0.3 * jax.random.normal(jax.random.fold_in(_rk, 611), (8, 256, 128), jnp.float32))
        _g = jax.random.normal(jax.random.fold_in(_rk, 9001), (2, 1), jnp.float32)
        _g = jnp.sign(_g) * jnp.maximum(jnp.abs(_g), 1.0) + (_g == 0) * 1.0
        g_xattn = _g[0]
        g_ffn = _g[1]
        return (x, ctx_512, g_xattn, g_ffn)
    x, ctx_512, g_xattn, g_ffn = _rec_inputs()

    def _L0_xattn_setup():
        import jax, jax.numpy as jnp
        import numpy as np
        N_HEADS = 16
        N_KV_HEADS = 4
        ROPE_THETA = 10000.0
        EPS = 1e-05

        def _rms_norm(x, w):
            var = jnp.mean(x * x, axis=-1, keepdims=True)
            return x * jax.lax.rsqrt(var + EPS) * w

        def _rope_sin_cos(T, head_dim, dtype):
            inv_freq = 1.0 / ROPE_THETA ** (jnp.arange(0, head_dim, 2, dtype=jnp.float32) / head_dim)
            t = jnp.arange(T, dtype=jnp.float32)
            freqs = jnp.outer(t, inv_freq)
            emb = jnp.concatenate([freqs, freqs], -1)
            return (jnp.sin(emb).astype(dtype)[None, None], jnp.cos(emb).astype(dtype)[None, None])

        def _rotate_half(x):
            h = x.shape[-1] // 2
            x1, x2 = (x[..., :h], x[..., h:])
            return jnp.concatenate([-x2, x1], axis=-1)
        key = jax.random.key(seed)
        ks = jax.random.split(key, 6)
        B, T, C = (2, 512, 512)
        Ckv = C // N_HEADS * N_KV_HEADS
        return {'q': jax.random.normal(ks[0], (B, T, C), jnp.float32), 'k': jax.random.normal(ks[1], (B, T, Ckv), jnp.float32), 'v': jax.random.normal(ks[2], (B, T, Ckv), jnp.float32), 'q_norm_w': jnp.ones((C,), jnp.float32), 'k_norm_w': jnp.ones((Ckv,), jnp.float32), 'w_out': jax.random.normal(ks[3], (C, C), jnp.float32) * C ** (-0.5)}
    _L0_xattn_all = _L0_xattn_setup()
    _L0_xattn_in = {k: v for k, v in _L0_xattn_all.items() if k in ('q_norm_w', 'k_norm_w', 'w_out')}
    del _L0_xattn_all

    def _L0_ffn_setup():
        import jax, jax.numpy as jnp
        import numpy as np
        TOPK = 4
        key = jax.random.key(seed)
        k_x, k_a, k_b, k_w, k_bias = jax.random.split(key, 5)
        b, s, h, j, a, r = (4, 512, 512, 512, 64, 16)
        x = jax.random.normal(k_x, (b, s, h), dtype=jnp.float32)
        A = jax.random.normal(k_a, (a, r, h), dtype=jnp.float32) * 0.02
        B = jax.random.normal(k_b, (a, j, r), dtype=jnp.float32) * 0.02
        W = jax.random.normal(k_w, (j, h), dtype=jnp.float32) * 0.02
        bias = jax.random.normal(k_bias, (j,), dtype=jnp.float32) * 0.02
        return {'x': x, 'A': A, 'B': B, 'W': W, 'bias': bias}
    _L0_ffn_all = _L0_ffn_setup()
    _L0_ffn_in = {k: v for k, v in _L0_ffn_all.items() if k in ('A', 'B', 'W', 'bias')}
    del _L0_ffn_all
    return {'x': x, 'ctx_512': ctx_512, 'g_xattn': g_xattn, 'g_ffn': g_ffn, 'L0_xattn_q_norm_w': _L0_xattn_in['q_norm_w'], 'L0_xattn_k_norm_w': _L0_xattn_in['k_norm_w'], 'L0_xattn_w_out': _L0_xattn_in['w_out'], 'L0_ffn_A': _L0_ffn_in['A'], 'L0_ffn_B': _L0_ffn_in['B'], 'L0_ffn_W': _L0_ffn_in['W'], 'L0_ffn_bias': _L0_ffn_in['bias']}

def reference(x, ctx_512, g_xattn, g_ffn, L0_xattn_q_norm_w, L0_xattn_k_norm_w, L0_xattn_w_out, L0_ffn_A, L0_ffn_B, L0_ffn_W, L0_ffn_bias):
    import jax
    import jax.numpy as jnp

    def _L0_xattn_ref(q, k, v, q_norm_w, k_norm_w, w_out):
        import jax, jax.numpy as jnp
        import numpy as np
        N_HEADS = 16
        N_KV_HEADS = 4
        ROPE_THETA = 10000.0
        EPS = 1e-05

        def _rms_norm(x, w):
            var = jnp.mean(x * x, axis=-1, keepdims=True)
            return x * jax.lax.rsqrt(var + EPS) * w

        def _rope_sin_cos(T, head_dim, dtype):
            inv_freq = 1.0 / ROPE_THETA ** (jnp.arange(0, head_dim, 2, dtype=jnp.float32) / head_dim)
            t = jnp.arange(T, dtype=jnp.float32)
            freqs = jnp.outer(t, inv_freq)
            emb = jnp.concatenate([freqs, freqs], -1)
            return (jnp.sin(emb).astype(dtype)[None, None], jnp.cos(emb).astype(dtype)[None, None])

        def _rotate_half(x):
            h = x.shape[-1] // 2
            x1, x2 = (x[..., :h], x[..., h:])
            return jnp.concatenate([-x2, x1], axis=-1)
        B, T, C = q.shape
        hd = C // N_HEADS
        g = N_HEADS // N_KV_HEADS
        q = _rms_norm(q, q_norm_w)
        k = _rms_norm(k, k_norm_w)
        q = q.reshape(B, T, N_HEADS, hd).transpose(0, 2, 1, 3)
        k = k.reshape(B, T, N_KV_HEADS, hd).transpose(0, 2, 1, 3)
        v = v.reshape(B, T, N_KV_HEADS, hd).transpose(0, 2, 1, 3)
        sin, cos = _rope_sin_cos(T, hd, q.dtype)
        q = q * cos + _rotate_half(q) * sin
        k = k * cos + _rotate_half(k) * sin
        qg = q.reshape(B, N_KV_HEADS, g, T, hd)
        scale = 1.0 / jnp.sqrt(jnp.asarray(hd, q.dtype))
        scores = jnp.einsum('bgnqd,bgkd->bgnqk', qg, k) * scale
        causal = jnp.tril(jnp.ones((T, T), bool))
        scores = jnp.where(causal, scores, jnp.asarray(-1e+30, scores.dtype))
        attn = jax.nn.softmax(scores, axis=-1)
        out = jnp.einsum('bgnqk,bgkd->bgnqd', attn, v)
        out = out.reshape(B, N_HEADS, T, hd).transpose(0, 2, 1, 3).reshape(B, T, C)
        return out @ w_out.T

    def _L0_ffn_ref(x, A, B, W, bias):
        import jax, jax.numpy as jnp
        import numpy as np
        TOPK = 4
        vecs = jnp.einsum('arh,bsh->bsar', A, x)
        arrows = jnp.linalg.norm(vecs, axis=-1)
        _, idx = jax.lax.top_k(arrows, TOPK)
        routes = jax.nn.one_hot(idx, arrows.shape[-1], dtype=x.dtype).sum(-2) / TOPK
        v = jnp.einsum('bsa,bsar->bsr', routes, vecs)
        delta = jnp.einsum('bsa,ajr,bsr->bsj', routes, B, v)
        base = jnp.einsum('bsh,jh->bsj', x, W) + bias
        return base + delta
    x = x + jnp.tanh(g_xattn[0]) * _L0_xattn_ref(_layernorm(x, axis=-1), ctx_512, ctx_512, L0_xattn_q_norm_w, L0_xattn_k_norm_w, L0_xattn_w_out)
    x = x + jnp.tanh(g_ffn[0]) * _L0_ffn_ref(_layernorm(x, axis=-1), L0_ffn_A, L0_ffn_B, L0_ffn_W, L0_ffn_bias)
    return x

_drawn_inputs = setup_inputs


def setup_inputs(seed=0):
    import zlib

    import numpy as np

    out = dict(_drawn_inputs(seed))
    spreads = {'L0_xattn_q_norm_w': (1.0, 0.2), 'L0_xattn_k_norm_w': (1.0, 0.2)}
    factors = {'L0_ffn_A': 4.133, 'L0_ffn_B': 3.396, 'L0_ffn_bias': 3.53}
    for name, (base, spread) in spreads.items():
        noise = np.random.default_rng([zlib.crc32(name.encode()), seed]).standard_normal(out[name].shape)
        drawn = base * np.exp(spread * noise) if base else spread * noise
        out[name] = jnp.asarray(drawn.astype(out[name].dtype))
    for name, factor in factors.items():
        out[name] = (out[name] * factor).astype(out[name].dtype)
    return out
```

```python
import numpy as np

import concourse.bass as bass
from concourse import mybir
from contextlib import ExitStack

F32 = mybir.dt.float32
F32R = mybir.dt.float32r
BF16 = mybir.dt.bfloat16
ALU = mybir.AluOpType
ACT = mybir.ActivationFunctionType
AX = mybir.AxisListType

P = 128
BATCHES, SEQ, DIM = 8, 256, 512
TILES = SEQ // P
HEADS, KV = 16, 4
HD = DIM // HEADS
GROUP = HEADS // KV
CTX = KV * HD
CHUNKS = DIM // P
ADAPTERS, RANK, TOPK = 64, 16, 4
PER_CHUNK = P // RANK
ROUTES = ADAPTERS // PER_CHUNK
EPS = 1e-5
SCALE = HD ** -0.5
NEG = -1e30
LOWEST = -3.0e38
SHIFT_ROW = 3 * HD

CONST_COLS = {}
_at = 0
for _name, _n in (("ident", P), ("spread_sum", P), ("pick", 2 * HD), ("mask", 2 * P), ("cos", TILES * HD),
                  ("sin", TILES * HD), ("expand", ROUTES * P)):
    CONST_COLS[_name] = (_at, _at + _n)
    _at += _n
N_CONST = _at
N_KEPT = CONST_COLS["mask"][1]

BANKS = 6


def _unit_order():
    u = [("F", "yT", 0), ("F", "yT", 1)]
    for v in range(4):
        u += [("A", "scores", 4 * v + k) for k in range(4)] + [("F", "vecs", v)]
    u += [("A", "maxT", 0), ("F", "ssq", 0), ("F", "normT", 0)]
    u += [("A", "st", n) for n in range(4)]
    u += [("F", "maskT", 0)] + [("F", "spread", v) for v in range(4)]
    u += [("A", "st", n) for n in range(4, 12)]
    u += [("A", "pv", 0), ("A", "pv", 1), ("N", "qkT", 0), ("N", "qkT", 1), ("N", "qkT", 2), ("F", "vsum", 0)]
    u += [("A", "pv", 2), ("A", "pv", 3), ("A", "proj", 0), ("A", "proj", 1)]
    return u


UNITS = _unit_order()
PLACE = {(kind, n): at for at, (_, kind, n) in enumerate(UNITS)}


def bank_of(kind, n):
    return PLACE[(kind, n)] % BANKS


def held_before(kind, n, here, before):
    at = PLACE[(kind, n)]
    for k in range(at - 1, -1, -1):
        if k % BANKS == at % BANKS and UNITS[k][0] in here:
            return (*UNITS[k], 0)
    for k in range(len(UNITS) - 1, -1, -1):
        if k % BANKS == at % BANKS and UNITS[k][0] in before:
            return (*UNITS[k], 1)
    return None


def build(nc, a):
    ctx = ExitStack()
    with ctx:
        def sb(name, shape, dt=F32):
            return ctx.enter_context(nc.sbuf_tensor(name, [P, *shape], dt))

        def sem(name):
            return ctx.enter_context(nc.semaphore(name))

        arena = (nc.sbuf_base + 31) // 32 * 32
        probs0 = sb("probs0", [KV, GROUP * P])
        probs1 = sb("probs1", [KV, 2, GROUP * P])
        half = KV * GROUP * P * 4
        o_hi = nc.alloc_sbuf_tensor_at("o_hi", [P, TILES, DIM], F32R, offset=arena)
        o_lo = nc.alloc_sbuf_tensor_at("o_lo", [P, TILES, DIM], F32R, offset=arena + half // 2)
        u_hi = nc.alloc_sbuf_tensor_at("u_hi", [P, ROUTES, SEQ], F32R, offset=arena + half)
        u_lo = nc.alloc_sbuf_tensor_at("u_lo", [P, ROUTES, SEQ], F32R, offset=arena + 2 * half)
        squares = probs1[:, :, :, :].rearrange("p g k c -> p (g k c)")[:, 0:ROUTES * SEQ].rearrange(
            "p (j t) -> p j t", j=ROUTES)
        expand_f = probs1[:, :, :, :].rearrange("p g k c -> p (g k c)")[:, 0:ROUTES * P]

        w_shape = {"o": (CHUNKS, DIM), "a": (CHUNKS, ADAPTERS * RANK), "w": (CHUNKS, DIM), "b": (ROUTES, DIM)}
        w_hi = {k: sb(f"w_{k}_hi", s, F32R) for k, s in w_shape.items()}
        w_lo = {k: sb(f"w_{k}_lo", s, F32R) for k, s in w_shape.items()}

        x_next = sb("x_next", [TILES, DIM])
        x_res = sb("x_res", [TILES, DIM])
        x_out = sb("x_out", [TILES, DIM])
        ctx_next = sb("ctx_next", [TILES, CTX])
        values = sb("values", [TILES, CTX])

        q_cos = sb("q_cos", [TILES, DIM])
        q_sin = sb("q_sin", [TILES, DIM])
        k_cos = sb("k_cos", [TILES, CTX])
        k_sin = sb("k_sin", [TILES, CTX])
        const = sb("const", [N_KEPT])
        ident, spread_sum, pick, mask = (const[:, slice(*CONST_COLS[k])]
                                         for k in ("ident", "spread_sum", "pick", "mask"))
        ident_bf = sb("ident_bf", [P], BF16)
        expand = sb("expand", [ROUTES, P], BF16)
        ones = sb("ones", [HD])
        gated_bias = sb("gated_bias", [DIM])
        gates = sb("gates", [2])
        minus_half = sb("minus_half", [2 * TILES])

        scratch = sb("scratch", [TILES, DIM])
        roped = sb("roped", [TILES, DIM])
        k_norm = sb("k_norm", [TILES, CTX])
        k_rope = sb("k_rope", [TILES, CTX])
        stats = sb("stats", [TILES, 6])
        aggr = sb("aggr", [TILES, 2])
        k_stats = sb("k_stats", [TILES, 6])
        k_aggr = sb("k_aggr", [TILES, 2])
        rms = sb("rms", [2, TILES])
        r_stats = sb("r_stats", [TILES, 6])
        r_aggr = sb("r_aggr", [TILES, 2])
        r_rms = sb("r_rms", [TILES])
        inverse = sb("inverse", [DIM // HD])
        q_stack = sb("q_stack", [HEADS, SEQ], F32R)
        k_stack = sb("k_stack", [KV, SEQ], F32R)
        maxima = sb("maxima", [TILES * HEADS])
        minus_max = sb("minus_max", [P])

        y_arena = (nc.sbuf_base + 31) // 32 * 32
        yT_hi = sb("yT_hi", [CHUNKS, SEQ], F32R)
        yT_lo = sb("yT_lo", [CHUNKS, SEQ], F32R)
        vecs = sb("vecs", [ROUTES, SEQ])
        q_hi, q_lo = vecs[:, 0:CHUNKS, :], vecs[:, CHUNKS:ROUTES, :]
        k_hi, k_lo = roped[:, 0, 0:SEQ], roped[:, 0, SEQ:2 * SEQ]
        spread = sb("spread", [ROUTES, SEQ], BF16)
        ssqT = sb("ssqT", [SEQ])
        norms = sb("norms", [TILES, ADAPTERS + 8])
        top = sb("top", [TILES, 8])
        wanted = sb("wanted", [TILES, 8])
        replaced = sb("replaced", [TILES, ADAPTERS + 8])
        chosen = sb("chosen", [TILES, P], BF16)
        chosenT = sb("chosenT", [SEQ], BF16)
        v_hi = sb("v_hi", [SEQ], F32R)
        v_lo = sb("v_lo", [SEQ], F32R)

        qw_b = vecs[:, 4:6, :].rearrange("p a b -> p (a b)")
        kw_b = vecs[:, 6, 0:CTX]
        trig = ssqT[:, 0:2 * TILES * HD]
        stage = [x_out[:, :, :].rearrange("p a b -> p (a b)"),
                 spread[:, :, :].rearrange("p a b -> p (a b)").bitcast(F32),
                 *(nc.alloc_sbuf_tensor_at(f"in_yT_{k}", [P, PIECE], F32, offset=y_arena + 4 * PIECE * k)[:, :]
                   for k in range(2)),
                 *(probs1[:, g, :, :].rearrange("p k c -> p (k c)") for g in range(1, KV))]

        banks = [ctx.enter_context(nc.psum_tensor(f"bank{k}", [P, 512], F32)) for k in range(BANKS)]
        acc = [ctx.enter_context(nc.psum_tensor(f"acc{t}", [P, 512], F32)) for t in range(TILES)]

        def bank(kind, n):
            return banks[bank_of(kind, n)]

        PER = dict(
            x_loaded=16, ctx_loaded=16, values_loaded=16, res_loaded=16, stacked0=96, stacked1=96, stacked2=96, stacked3=96, shift_stacked=32,
            x_out_free=32,
            yT_done=2, scores_done=16, vecs_done=4, ssq_done=1, maxT_done=1, normT_done=1, st_done=12,
            maskT_done=1, spread_done=4, pv_done=4, vsum_done=1, qkT_done=3, proj_done=2, acc_done=2,
            yT_hi_ready=2, vecs_ready=4, squared=4, ssqT_ready=1, minus_ready=1, exp_done=12, chosenT_ready=1,
            spread_ready=4, o_hi_ready=2, v_hi_ready=1, qk_hi_ready=3,
            yT_lo_ready=2, maxed=32, norms_taken=1, routed=1, stat_step=10, q_step=8, k_step=5, q_roped=2, k_roped=1, picked=4,
            vsum_ready=1, sums_taken=2, norm_step=4, quotient_ready=2, o_lo_ready=2, v_lo_ready=1, u_hi_ready=2, qk_lo_ready=3,
            x1_ready=2, y_step=4, rms_ready=1, var_ready=2, y_ready=2, out_ready=2, route_step=5,
            biased=1, masked=8, rooted=1, y_rooted=2, u_lo_ready=2)
        ONCE = ("const_loaded", "trig_loaded", "expand_loaded", "vectors_loaded", "gates_loaded", "w_hi_done",
                "w_lo_by_pool", "w_lo_by_dve", *(f"w{s}_loaded" for s in range(len(stage))), "tables", "gated", "constants", "expand_ready", "fills", "exponents")
        S = {k: sem(k) for k in (*PER, *ONCE)}

        def wait(eng, name, batch, done=None):
            eng.wait_ge(S[name], PER[name] * batch + (PER[name] if done is None else done))

        def settled_wait(eng, name, batch, done=None):
            value = PER[name] * batch + (PER[name] if done is None else done)
            if not isinstance(batch, int):
                value = eng.compute_val(value)
                eng.wait_ge(S[name], 1)
            eng.wait_ge(S[name], value)

        def split_lo(eng, c):
            s = c % len(stage)
            eng.wait_ge(S["w_hi_done"], c + 1)
            ins = eng.tensor_tensor(w_part(w_lo, c), stage[s], w_part(w_hi, c).bitcast(F32), ALU.subtract)
            if c == X_OUT_LAST:
                ins.then_inc(S["x_out_free"], 32)
            else:
                ins.then_inc(S["w_lo_by_pool" if c in LO_BY_POOL else "w_lo_by_dve"], 1)

        def wait_split(eng, c):
            if c == X_OUT_LAST:
                eng.wait_ge(S["x_out_free"], 32)
            elif c in LO_BY_POOL:
                eng.wait_ge(S["w_lo_by_pool"], LO_BY_POOL.index(c) + 1)
            else:
                eng.wait_ge(S["w_lo_by_dve"], LO_BY_DVE.index(c) + 1)

        def wait_all_split(eng):
            eng.wait_ge(S["x_out_free"], 32)
            eng.wait_ge(S["w_lo_by_pool"], len(LO_BY_POOL) - 1)
            eng.wait_ge(S["w_lo_by_dve"], len(LO_BY_DVE))

        READ = {"yT": lambda n: ("yT_lo_ready", n + 1), "scores": lambda n: ("maxed", 2 * n + 2),
                "vecs": lambda n: ("squared", n + 1), "ssq": lambda n: ("ssqT_ready", 1),
                "maxT": lambda n: ("minus_ready", 1), "normT": lambda n: ("norms_taken", 1),
                "st": lambda n: ("exp_done", n + 1), "maskT": lambda n: ("chosenT_ready", 1),
                "spread": lambda n: ("spread_ready", n + 1),
                "pv": lambda n: (("sums_taken", "quotient_ready")[n % 2], n // 2 + 1),
                "vsum": lambda n: ("v_lo_ready", 1), "qkT": lambda n: ("qk_lo_ready", n + 1),
                "proj": lambda n: ("x1_ready", n + 1)}
        AHEAD = {"A": 0, "F": -1, "N": 1}

        def tile_of(u):
            return (u, 0, 0) if u < KV else ((u - KV) // 2, 1 - (u - KV) % 2, 1)

        def chain(eng, name, batch):
            count = [0]

            def did(ins, last=False):
                count[0] += 1
                assert count[0] <= PER[name]
                ins.then_inc(S[name], 1)

            def settle():
                wait(eng, name, batch, count[0])
            return did, settle

        def halves(ap, s):
            return ap.rearrange("p (g n s d) -> p g n s d", g=KV, s=2, d=HD // 2)[:, :, :, s, :]

        def run(eng, step):
            step(-1, "N", "")
            step(0, "AN", "N")
            with eng.Fori(1, BATCHES - 1) as i:
                step(i, "FAN", "AN")
            step(BATCHES - 1, "FA", "FAN")
            step(BATCHES, "F", "FA")

        block = ctx.enter_context(nc.Block())

        @block.sync
        def _(sp):
            def load_values(b):
                sp.dma_start(values[:, :, :], a["ctx"][b].rearrange("(t p) c -> p t c", p=P)
                             ).then_inc(S["values_loaded"], 16)

            def load_res(b):
                sp.dma_start(x_res[:, :, :], a["x"][b].rearrange("(t p) c -> p t c", p=P)
                             ).then_inc(S["res_loaded"], 16)

            def step(i, here, before):
                if here == "N":
                    sp.dma_start(trig, a["const"][:, CONST_COLS["cos"][0]:CONST_COLS["sin"][1]]
                                 ).then_inc(S["trig_loaded"], 16)
                    sp.dma_start(qw_b, a["qw"].broadcast_to([P, DIM])).then_inc(S["vectors_loaded"], 16)
                    sp.dma_start(kw_b, a["kw"].broadcast_to([P, CTX])).then_inc(S["vectors_loaded"], 16)
                    sp.dma_start(const[:, :], a["const"][:, 0:N_KEPT]).then_inc(S["const_loaded"], 16)
                    sp.dma_start(gates[:, 0:1], a["g_x"].broadcast_to([P, 1])).then_inc(S["gates_loaded"], 16)
                    sp.dma_start(gates[:, 1:2], a["g_f"].broadcast_to([P, 1])).then_inc(S["gates_loaded"], 16)
                    sp.dma_start(gated_bias[:, :], a["bias"].broadcast_to([P, DIM])).then_inc(S["gates_loaded"], 16)
                    sp.dma_start(expand_f, a["const"][:, slice(*CONST_COLS["expand"])]
                                 ).then_inc(S["expand_loaded"], 16)
                if "A" in here:
                    if "A" in before:
                        wait(sp, "pv_done", i - 1)
                    load_values(i)
                    if "F" in here:
                        wait(sp, "biased", i - 1)
                        wait(sp, "y_ready", i - 1)
                    load_res(i)
                    wait(sp, "minus_ready", i)
                    for t in range(TILES):
                        sp.dma_start(q_stack[SHIFT_ROW:SHIFT_ROW + 1, :, t * P:(t + 1) * P].bitcast(F32),
                                     minus_max[t * HEADS:(t + 1) * HEADS, :]).then_inc(S["shift_stacked"], 16)
                if "N" in here:
                    wait(sp, "qk_lo_ready", i + 1)
                    for g in range(KV):
                        rows = slice(g * HD, (g + 1) * HD)
                        for part, (qs, ks) in enumerate(((q_hi, k_hi), (q_lo, k_hi), (q_hi, k_lo))):
                            to = slice(part * HD, (part + 1) * HD)
                            sp.dma_start(q_stack[to, g * GROUP:(g + 1) * GROUP, :].bitcast(F32), qs[rows]
                                         ).then_inc(S[f"stacked{g}"], 16)
                            sp.dma_start(k_stack[to, g, :].bitcast(F32), ks[rows]).then_inc(S[f"stacked{g}"], 16)
                if "F" in here:
                    for t in range(TILES):
                        wait(sp, "out_ready", i - 1, t + 1)
                        sp.dma_start(a["out"][i - 1][t * P:(t + 1) * P, :], x_out[:, t, :]
                                     ).then_inc(S["x_out_free"], 16)

            run(sp, step)
            wait(sp, "x_out_free", BATCHES)

        @block.tensor
        def _(pe):
            def step(i, here, before):
                def take(kind, n, implied=None):
                    held = held_before(kind, n, here, before)
                    if held:
                        stage_, k, m, ago = held
                        name, count = READ[k](m)
                        if name != implied:
                            wait(pe, name, i + AHEAD[stage_] - ago, count)
                    return bank(kind, n)

                def products(out, terms, name, first=True, last=True):
                    for k, (l, r) in enumerate(terms):
                        ins = nc.tensor.matmul(out, l, r, start=(first and k == 0),
                                               stop=(last and k == len(terms) - 1), skip_group_check=True)
                    if name:
                        ins.then_inc(S[name], 1)

                f, n = i - 1, i + 1

                def y_transposed(t):
                    wait(pe, "y_ready", f, t + 1)
                    ps = take("yT", t)
                    for c in range(CHUNKS):
                        ins = nc.tensor.transpose(ps[:, c * P:(c + 1) * P], scratch[:, t, c * P:(c + 1) * P], ident)
                    ins.then_inc(S["yT_done"], 1)

                def scores(u):
                    if u in (0, 2, 4, 6):
                        wait(pe, f"stacked{u // 2}", i)
                    ps = take("scores", u)
                    t = u // (HEADS // 2)
                    for k in range(2):
                        h = 2 * (u % (HEADS // 2)) + k
                        ins = nc.tensor.matmul(ps[:, k * SEQ:(k + 1) * SEQ],
                                               q_stack[0:SHIFT_ROW, h, t * P:(t + 1) * P],
                                               k_stack[0:SHIFT_ROW, h // GROUP, :], start=True, stop=True)
                    ins.then_inc(S["scores_done"], 1)

                def adapter_vecs(v):
                    if v == 0:
                        wait(pe, "yT_lo_ready", f)
                    ps = take("vecs", v, "yT_lo_ready")
                    for k in range(2):
                        cols = slice((2 * v + k) * P, (2 * v + k + 1) * P)
                        terms = [(w[:, c, cols], y[:, c, :]) for w, y in
                                 ((w_hi["a"], yT_hi), (w_lo["a"], yT_hi), (w_hi["a"], yT_lo)) for c in range(CHUNKS)]
                        products(ps[:, k * SEQ:(k + 1) * SEQ], terms, "vecs_done" if k else None)

                def squared_norms():
                    wait(pe, "squared", f)
                    ps = take("ssq", 0)
                    for parity in range(2):
                        for q in range(4):
                            ins = nc.tensor.matmul(ps[q * HD:(q + 1) * HD, 0:SEQ],
                                                   pick[:, parity * HD:(parity + 1) * HD],
                                                   squares[:, 2 * q + parity, :], start=(parity == 0),
                                                   stop=(parity == 1), skip_group_check=True)
                    ins.then_inc(S["ssq_done"], 1)

                def norms_transposed():
                    wait(pe, "ssqT_ready", f)
                    ps = take("normT", 0)
                    for t in range(TILES):
                        ins = nc.tensor.transpose(ps[:, t * P:(t + 1) * P], ssqT[:, t * P:(t + 1) * P], ident)
                    ins.then_inc(S["normT_done"], 1)

                def maxima_transposed():
                    wait(pe, "maxed", i)
                    ps = take("maxT", 0)
                    nc.tensor.transpose(ps[0:TILES * HEADS, 0:P], maxima[:, :], ident).then_inc(S["maxT_done"], 1)

                def base(t, start, end):
                    toks = slice(t * P, (t + 1) * P)
                    terms = [(y[:, c, toks], w[:, c, :]) for y, w in
                             ((yT_hi, w_hi["w"]), (yT_lo, w_hi["w"]), (yT_hi, w_lo["w"])) for c in range(CHUNKS)]
                    products(acc[t][:, :], terms[start:end], None, first=(start == 0), last=False)

                def scores_T(u):
                    if u == 0:
                        wait(pe, "shift_stacked", i)
                    ps = take("st", u)
                    g, kb, t = tile_of(u)
                    nc.tensor.matmul(ps[:, :], k_stack[0:SHIFT_ROW + 1, g, kb * P:(kb + 1) * P],
                                     q_stack[0:SHIFT_ROW + 1, g * GROUP:(g + 1) * GROUP, t * P:(t + 1) * P],
                                     start=True, stop=True).then_inc(S["st_done"], 1)

                def mask_transposed():
                    wait(pe, "routed", f)
                    ps = take("maskT", 0)[:, :].bitcast(BF16)
                    for t in range(TILES):
                        ins = nc.tensor.transpose(ps[:, t * P:(t + 1) * P], chosen[:, t, :], ident_bf[:, :])
                    ins.then_inc(S["maskT_done"], 1)

                def mask_spread(v):
                    if v == 0:
                        wait(pe, "chosenT_ready", f)
                    ps = take("spread", v)
                    for k in range(2):
                        ins = nc.tensor.matmul(ps[:, k * SEQ:(k + 1) * SEQ], expand[:, 2 * v + k, :], chosenT[:, :],
                                               start=True, stop=True)
                    ins.then_inc(S["spread_done"], 1)

                def attend(u):
                    t, with_values = u // 2, u % 2
                    if u == 0:
                        wait(pe, "values_loaded", i)
                    if not with_values:
                        wait(pe, "masked", i, 4 * (t + 1))
                        wait(pe, "exp_done", i, (4, 12)[t])
                    ps = take("pv", u)
                    for kb in range(t + 1):
                        for g in range(KV):
                            pr = probs1[:, g, kb, :] if t else probs0[:, g, :]
                            l = values[:, kb, g * HD:(g + 1) * HD] if with_values else ones[:, :]
                            ins = nc.tensor.matmul(ps[g * HD:(g + 1) * HD, :], l, pr, start=(kb == 0),
                                                   stop=(kb == t), skip_group_check=True)
                    ins.then_inc(S["pv_done"], 1)

                def chosen_sum():
                    wait(pe, "vsum_ready", f)
                    ps = take("vsum", 0)
                    nc.tensor.matmul(ps[:, 0:SEQ], spread_sum, ssqT[:, :], start=True, stop=True
                                     ).then_inc(S["vsum_done"], 1)

                def qk_transposed(u):
                    if u < TILES:
                        wait(pe, "q_roped", n, u + 1)
                    else:
                        wait(pe, "k_roped", n)
                    ps = take("qkT", u)
                    for c in range(CHUNKS if u < TILES else TILES):
                        src = roped[:, u, c * P:(c + 1) * P] if u < TILES else k_rope[:, c, :]
                        ins = nc.tensor.transpose(ps[:, c * P:(c + 1) * P], src, ident)
                    ins.then_inc(S["qkT_done"], 1)

                def project(t):
                    wait(pe, "o_hi_ready", i, t + 1)
                    ps = take("proj", t)
                    terms = [(o[:, t, c * P:(c + 1) * P], w[:, c, :]) for o, w in
                             ((o_hi, w_hi["o"]), (o_hi, w_lo["o"]), (o_lo, w_hi["o"])) for c in range(CHUNKS)]
                    products(ps[:, :], terms[:2 * CHUNKS], None, last=False)
                    wait(pe, "o_lo_ready", i, t + 1)
                    products(ps[:, :], terms[2 * CHUNKS:], "proj_done", first=False)

                def delta(t):
                    toks = slice(t * P, (t + 1) * P)
                    for k in range(2):
                        if t == 0:
                            wait(pe, "u_hi_ready", f, k + 1)
                        products(acc[t][:, :], [(u_hi[:, j, toks], w[:, j, :]) for w in (w_hi["b"], w_lo["b"])
                                                for j in range(4 * k, 4 * k + 4)], None, first=False, last=False)
                    if t == 0:
                        wait(pe, "u_lo_ready", f)
                    products(acc[t][:, :], [(u_lo[:, j, toks], w_hi["b"][:, j, :]) for j in range(ROUTES)],
                             "acc_done", first=False)

                if here == "N":
                    pe.wait_ge(S["const_loaded"], 16)
                    pe.wait_ge(S["constants"], 1)
                    pe.wait_ge(S["fills"], 5)
                F, A, N = "F" in here, "A" in here, "N" in here
                if F:
                    y_transposed(0)
                    y_transposed(1)
                for v in range(4):
                    if A:
                        for k in range(4):
                            scores(4 * v + k)
                    if F:
                        adapter_vecs(v)
                if F:
                    base(0, 0, 4)
                if A:
                    maxima_transposed()
                if F:
                    base(0, 4, 12)
                    squared_norms()
                    base(1, 0, 4)
                    norms_transposed()
                if A:
                    for u in range(4):
                        scores_T(u)
                if F:
                    mask_transposed()
                    base(1, 4, 12)
                    for v in range(4):
                        mask_spread(v)
                if A:
                    for u in range(4, 12):
                        scores_T(u)
                    attend(0)
                    attend(1)
                if N:
                    for u in range(3):
                        qk_transposed(u)
                if F:
                    chosen_sum()
                if A:
                    attend(2)
                    attend(3)
                if here == "AN":
                    wait_all_split(pe)
                    pe.wait_ge(S["expand_ready"], 1)
                if A:
                    project(0)
                    project(1)
                if F:
                    delta(0)
                    delta(1)

            run(pe, step)

        @block.scalar
        def _(act):
            def load_x(n):
                nc.scalar.dma_start(x_next[:, :, :], a["x"][n].rearrange("(t p) c -> p t c", p=P)
                                    ).then_inc(S["x_loaded"], 16)
                nc.scalar.dma_start(ctx_next[:, :, :], a["ctx"][n].rearrange("(t p) c -> p t c", p=P)
                                    ).then_inc(S["ctx_loaded"], 16)

            def load_weights(c):
                s = c % len(stage)
                if c >= len(stage):
                    wait_split(act, c - len(stage))
                nc.scalar.dma_start(stage[s], a["weights"][c]).then_inc(S[f"w{s}_loaded"], 16)

            def split_hi(c):
                act.wait_ge(S[f"w{c % len(stage)}_loaded"], 16 * (c // len(stage) + 1))
                nc.scalar.copy(w_part(w_hi, c), stage[c % len(stage)]).then_inc(S["w_hi_done"], 1)

            def step(i, here, before):
                f, n = i - 1, i + 1

                def exponentials(u):
                    g, kb, t = tile_of(u)
                    to = probs1[:, g, kb, :] if t else probs0[:, g, :]
                    wait(act, "st_done", i, u + 1)
                    nc.scalar.activation(to, bank("st", u)[:, :], ACT.Exp).then_inc(S["exp_done"], 1)

                def quotient_hi(t):
                    wait(act, "quotient_ready", i, t + 1)
                    nc.scalar.copy(o_hi[:, t, :], scratch[:, 1, :]).then_inc(S["o_hi_ready"], 1)

                if here == "N":
                    load_x(0)
                    for c in range(len(stage)):
                        load_weights(c)
                    act.wait_ge(S["gates_loaded"], 48)
                    nc.scalar.activation(gates[:, :], gates[:, :], ACT.Tanh).then_inc(S["gated"], 1)
                    for c in range(4):
                        split_hi(c)
                elif "N" in here:
                    wait(act, "k_roped", i)
                    load_x(n)
                if here == "AN":
                    act.wait_ge(S["expand_loaded"], 16)
                    nc.scalar.copy(expand[:, :, :].rearrange("p j c -> p (j c)"), expand_f
                                   ).then_inc(S["expand_ready"], 1)
                    for c in range(4, len(W_PIECES)):
                        if c + 3 < len(W_PIECES):
                            load_weights(c + 3)
                        split_hi(c)
                if "F" in here:
                    for t in range(TILES):
                        wait(act, "yT_done", f, t + 1)
                        nc.scalar.copy(yT_hi[:, :, t * P:(t + 1) * P],
                                       bank("yT", t)[:, :].rearrange("p (c q) -> p c q", c=CHUNKS)
                                       ).then_inc(S["yT_hi_ready"], 1)
                    for v in range(4):
                        ps = bank("vecs", v)[:, :].rearrange("p (k t) -> p k t", k=2)
                        wait(act, "vecs_done", f, v + 1)
                        if v == 0 and "A" in here:
                            for g in range(KV):
                                wait(act, f"stacked{g}", i)
                        nc.scalar.copy(vecs[:, 2 * v:2 * v + 2, :], ps).then_inc(S["vecs_ready"], 1)
                        nc.scalar.activation(squares[:, 2 * v:2 * v + 2, :], ps, ACT.Square).then_inc(S["squared"], 1)
                if "A" in here:
                    wait(act, "maxT_done", i)
                    nc.scalar.mul(minus_max[0:TILES * HEADS, :].bitcast(F32R), bank("maxT", 0)[0:TILES * HEADS, 0:P],
                                  -1.0).then_inc(S["minus_ready"], 1)
                if "F" in here:
                    wait(act, "ssq_done", f)
                    nc.scalar.copy(ssqT[:, :], bank("ssq", 0)[:, 0:SEQ]).then_inc(S["ssqT_ready"], 1)
                if "A" in here:
                    for u in range(4):
                        exponentials(u)
                if "F" in here:
                    wait(act, "maskT_done", f)
                    nc.scalar.copy(chosenT[:, :], bank("maskT", 0)[:, :].bitcast(BF16)[:, 0:SEQ]
                                   ).then_inc(S["chosenT_ready"], 1)
                    for v in range(4):
                        wait(act, "spread_done", f, v + 1)
                        nc.scalar.copy(spread[:, 2 * v:2 * v + 2, :],
                                       bank("spread", v)[:, :].rearrange("p (k t) -> p k t", k=2)
                                       ).then_inc(S["spread_ready"], 1)
                if here == "AN":
                    wait_all_split(act)
                if "A" in here:
                    for u in range(4, 12):
                        exponentials(u)
                if "A" in here:
                    quotient_hi(0)
                if "F" in here:
                    wait(act, "vsum_done", f)
                    nc.scalar.copy(v_hi[:, :], bank("vsum", 0)[:, 0:SEQ]).then_inc(S["v_hi_ready"], 1)
                if "N" in here:
                    for t in range(TILES):
                        wait(act, "qkT_done", n, t + 1)
                        if t == 0 and "F" in here:
                            wait(act, "vsum_ready", f)
                        nc.scalar.copy(q_hi[:, :, t * P:(t + 1) * P].bitcast(F32R),
                                       bank("qkT", t)[:, :].rearrange("p (c q) -> p c q", c=CHUNKS)
                                       ).then_inc(S["qk_hi_ready"], 1)
                    wait(act, "qkT_done", n)
                    nc.scalar.copy(k_hi.bitcast(F32R), bank("qkT", 2)[:, 0:SEQ]).then_inc(S["qk_hi_ready"], 1)
                if "A" in here:
                    quotient_hi(1)

            run(act, step)

        @block.vector
        def _(dve):
            def tables():
                cos, sin = (trig[:, k * TILES * HD:(k + 1) * TILES * HD] for k in range(2))
                todo = []
                for heads, w, to_cos, to_sin in ((HEADS, qw_b, q_cos, q_sin), (KV, kw_b, k_cos, k_sin)):
                    hd = HD // 2
                    for t in range(TILES):
                        at = lambda ap, s: ap.rearrange("p (h s d) -> p h s d", h=heads, s=2)[:, :, s, :]
                        wide = lambda ap, s: ap[:, t * HD + s * hd:t * HD + (s + 1) * hd].unsqueeze(1).broadcast_to(
                            [P, heads, hd])
                        for s in range(2):
                            todo.append((at(to_cos[:, t, :], s), at(w, s), wide(cos, s)))
                            todo.append((at(to_sin[:, t, :], s), at(w, 1 - s), wide(sin, s)))
                for out, l, r in todo:
                    dve.tensor_tensor(out, l, r, ALU.mult).then_inc(S["tables"], 1)
                return len(todo)

            def statistics(n):
                did, settle = chain(dve, "stat_step", n)
                wait(dve, "x_loaded", n)
                for t in range(TILES):
                    did(dve.bn_stats(stats[:, t, :], x_next[:, t, :]))
                wait(dve, "ctx_loaded", n)
                for t in range(TILES):
                    did(dve.bn_stats(k_stats[:, t, :], ctx_next[:, t, :]))
                settled_wait(dve, "stat_step", n, 4)
                for t in range(TILES):
                    did(dve.bn_aggr(aggr[:, t, :], stats[:, t, :]))
                    did(dve.bn_aggr(k_aggr[:, t, :], k_stats[:, t, :]))
                settle()
                did(dve.tensor_scalar(rms[:, 0, :], aggr[:, :, 1], HD * (1.0 + EPS), HD * EPS * EPS,
                                      ALU.mult, ALU.add))
                did(dve.tensor_tensor(rms[:, 1, :], k_aggr[:, :, 0], k_aggr[:, :, 0], ALU.mult))
                settle()
                dve.scalar_tensor_tensor(out=rms[:, 1, :], in0=k_aggr[:, :, 1], scalar=EPS, in1=rms[:, 1, :],
                                         op0=ALU.add, op1=ALU.add).then_inc(S["rms_ready"], 1)

            normed, product = scratch[:, 0, :], scratch[:, 1, :]

            def rotate_queries(n, t):
                out = roped[:, t, :].rearrange("p (n g d) -> p g n d", n=GROUP, g=KV)
                heads = lambda ap: ap.rearrange("p (g n d) -> p g n d", g=KV, n=GROUP)
                if t == 0:
                    wait(dve, "rooted", n)
                dve.tensor_scalar(normed, x_next[:, t, :], aggr[:, t, 0:1], rms[:, 0, t:t + 1],
                                  ALU.subtract, ALU.mult).then_inc(S["q_step"], 1)
                wait(dve, "q_step", n, 4 * t + 1)
                dve.tensor_tensor(out, heads(normed), heads(q_cos[:, t, :]), ALU.mult).then_inc(S["q_step"], 1)
                for s in range(2):
                    dve.tensor_tensor(halves(product, s), halves(normed, 1 - s), halves(q_sin[:, t, :], s),
                                      ALU.mult).then_inc(S["q_step"], 1)
                wait(dve, "q_step", n, 4 * t + 4)
                dve.tensor_tensor(out, out, heads(product), ALU.add).then_inc(S["q_roped"], 1)

            def rotate_keys(n):
                did, settle = chain(dve, "k_step", n)
                for t in range(TILES):
                    did(dve.tensor_scalar(k_norm[:, t, :], ctx_next[:, t, :], rms[:, 1, t:t + 1], None, ALU.mult))
                settle()
                flat = lambda ap: ap[:, :, :].rearrange("p t c -> p (t c)")
                swap = lambda ap, s: ap.rearrange("p (h s d) -> p h s d", s=2, d=HD // 2)[:, :, s, :]
                did(dve.tensor_tensor(flat(k_rope), flat(k_norm), flat(k_cos), ALU.mult))
                wait(dve, "q_roped", n)
                for s in range(2):
                    did(dve.tensor_tensor(swap(product[:, 0:TILES * CTX], s), swap(flat(k_norm), 1 - s),
                                          swap(flat(k_sin), s), ALU.mult))
                settle()
                dve.tensor_tensor(flat(k_rope), flat(k_rope), product[:, 0:TILES * CTX], ALU.add
                                  ).then_inc(S["k_roped"], 1)

            def maxima_of(b, units):
                for u in units:
                    t, ps = u // (HEADS // 2), bank("scores", u)
                    settled_wait(dve, "scores_done", b, u + 1)
                    if u >= 4:
                        settled_wait(dve, "maxed", b, 2 * u - 6)
                    for k in range(2):
                        h, keys = 2 * (u % (HEADS // 2)) + k, (t + 1) * P
                        slot = probs0[:, u % 4, k * SEQ:k * SEQ + keys]
                        dve.tensor_tensor_reduce(slot, ps[:, k * SEQ:k * SEQ + keys],
                                                 mask[:, 2 * P - keys:2 * P], 1.0, LOWEST, ALU.add, ALU.max,
                                                 maxima[:, t * HEADS + h:t * HEADS + h + 1]).then_inc(S["maxed"], 1)

            def route(f):
                did, settle = chain(dve, "route_step", f)
                wait(dve, "normT_done", f)
                dve.tensor_copy(norms[:, :, 0:ADAPTERS].rearrange("p t (q a) -> p t q a", q=4),
                                bank("normT", 0)[:, 0:TILES * P].rearrange("p (t q a) -> p t q a", t=TILES, q=4
                                                                          )[:, :, :, 0:RANK]
                                ).then_inc(S["norms_taken"], 1)
                settled_wait(dve, "norms_taken", f)
                for t in range(TILES):
                    did(dve.max(top[:, t, :], norms[:, t, 0:ADAPTERS]))
                settle()
                did(dve.tensor_copy(wanted[:, :, 0:TOPK], top[:, :, 0:TOPK]))
                settled_wait(dve, "route_step", f, 3)
                for t in range(TILES):
                    did(dve.match_replace(replaced[:, t, :], wanted[:, t, :], norms[:, t, :], -2.0))
                settle()
                dve.tensor_scalar(chosen[:, :, :].rearrange("p t (q a) -> p t q a", q=4)[:, :, :, 0:RANK],
                                  replaced[:, :, 0:ADAPTERS].rearrange("p t (q a) -> p t q a", q=4),
                                  -1.5, None, ALU.is_lt).then_inc(S["routed"], 1)

            def choose(f):
                for v in range(4):
                    wait(dve, "spread_ready", f, v + 1)
                    if v == 0:
                        wait(dve, "vecs_ready", f)
                    part = vecs[:, 2 * v:2 * v + 2, :]
                    dve.tensor_tensor(part, part, spread[:, 2 * v:2 * v + 2, :], ALU.mult).then_inc(S["picked"], 1)
                wait(dve, "picked", f)
                dve.tensor_reduce(ssqT[:, :], vecs[:, :, :].rearrange("p j t -> p t j"), AX.X, ALU.add
                                  ).then_inc(S["vsum_ready"], 1)

            def quotient(b, t):
                sums = scratch[:, 0, :]
                wait(dve, "pv_done", b, 2 * t + 1)
                dve.transpose(sums, bank("pv", 2 * t)[:, :]).then_inc(S["sums_taken"], 1)
                wait(dve, "sums_taken", b, t + 1)
                dve.reciprocal(inverse[:, :], sums.rearrange("p (k r) -> p k r", r=HD)[:, :, 0]
                               ).then_inc(S["norm_step"], 1)
                wait(dve, "norm_step", b, 2 * t + 1)
                dve.transpose(sums, inverse[:, :].unsqueeze(2).broadcast_to([P, DIM // HD, HD])
                              ).then_inc(S["norm_step"], 1)
                wait(dve, "norm_step", b, 2 * t + 2)
                wait(dve, "pv_done", b, 2 * t + 2)
                if t:
                    wait(dve, "o_hi_ready", b, t)
                dve.tensor_tensor(scratch[:, 1, :], bank("pv", 2 * t + 1)[:, :], sums, ALU.mult
                                  ).then_inc(S["quotient_ready"], 1)

            def quotient_lo(b, t):
                wait(dve, "o_hi_ready", b, t + 1)
                dve.tensor_tensor(o_lo[:, t, :], scratch[:, 1, :], o_hi[:, t, :].bitcast(F32), ALU.subtract
                                  ).then_inc(S["o_lo_ready"], 1)

            def v_low(f):
                wait(dve, "v_hi_ready", f)
                dve.tensor_tensor(v_lo[:, :], bank("vsum", 0)[:, 0:SEQ], v_hi[:, :].bitcast(F32), ALU.subtract
                                  ).then_inc(S["v_lo_ready"], 1)

            def spread_v(f, b):
                if b is not None:
                    wait(dve, "pv_done", b)
                for k in range(2):
                    js = slice(4 * k, 4 * k + 4)
                    dve.tensor_tensor(u_hi[:, js, :], spread[:, js, :],
                                      v_hi[:, :].bitcast(F32).unsqueeze(1).broadcast_to([P, 4, SEQ]), ALU.mult
                                      ).then_inc(S["u_hi_ready"], 1)

            def residual(b):
                did, settle = chain(dve, "y_step", b)
                for t in range(TILES):
                    wait(dve, "proj_done", b, t + 1)
                    if t == 0:
                        wait(dve, "res_loaded", b)
                    dve.scalar_tensor_tensor(out=x_res[:, t, :], in0=bank("proj", t)[:, :], scalar=gates[:, 0:1],
                                             in1=x_res[:, t, :], op0=ALU.mult, op1=ALU.add
                                             ).then_inc(S["x1_ready"], 1)
                    wait(dve, "x1_ready", b, t + 1)
                    did(dve.bn_stats(r_stats[:, t, :], x_res[:, t, :]))
                    settled_wait(dve, "y_step", b, 2 * t + 1)
                    did(dve.bn_aggr(r_aggr[:, t, :], r_stats[:, t, :]))
                    settle()
                    dve.tensor_scalar(r_rms[:, t:t + 1], r_aggr[:, t, 1:2], EPS, None, ALU.add
                                      ).then_inc(S["var_ready"], 1)
                    wait(dve, "y_rooted", b, t + 1)
                    dve.tensor_scalar(scratch[:, t, :], x_res[:, t, :], r_aggr[:, t, 0:1], r_rms[:, t:t + 1],
                                      ALU.subtract, ALU.mult).then_inc(S["y_ready"], 1)

            def result(f):
                wait(dve, "biased", f)
                for t in range(TILES):
                    wait(dve, "acc_done", f, t + 1)
                    dve.scalar_tensor_tensor(out=x_out[:, t, :], in0=acc[t][:, :], scalar=gates[:, 1:2],
                                             in1=x_out[:, t, :], op0=ALU.mult, op1=ALU.add
                                             ).then_inc(S["out_ready"], 1)

            def step(i, here, before):
                f, n = i - 1, i + 1
                if here == "N":
                    dve.memset(ones[:, :], 1.0).then_inc(S["fills"], 1)
                    dve.memset(k_stack[SHIFT_ROW:SHIFT_ROW + 1, :, :].bitcast(F32), 1.0).then_inc(S["fills"], 1)
                    dve.memset(norms[:, :, ADAPTERS:], -1.0).then_inc(S["fills"], 1)
                    dve.memset(wanted[:, :, :], -1.0).then_inc(S["fills"], 1)
                    dve.memset(chosen[:, :, :], 0.0).then_inc(S["fills"], 1)
                    dve.wait_ge(S["fills"], 5)
                    dve.wait_ge(S["const_loaded"], 16)
                    dve.tensor_copy(ident_bf[:, :], ident).then_inc(S["constants"], 1)
                    statistics(n)
                    dve.wait_ge(S["trig_loaded"], 16)
                    dve.wait_ge(S["vectors_loaded"], 32)
                    dve.wait_ge(S["tables"], tables())
                if "F" in here:
                    for t in range(TILES):
                        wait(dve, "yT_hi_ready", f, t + 1)
                        cols = slice(t * P, (t + 1) * P)
                        dve.tensor_tensor(yT_lo[:, :, cols],
                                          bank("yT", t)[:, :].rearrange("p (c q) -> p c q", c=CHUNKS),
                                          yT_hi[:, :, cols].bitcast(F32), ALU.subtract
                                          ).then_inc(S["yT_lo_ready"], 1)
                if "A" in here:
                    if "N" in here:
                        statistics(n)
                    maxima_of(i, range(0, 8))
                if "N" in here:
                    rotate_queries(n, 0)
                if "A" in here:
                    maxima_of(i, range(8, HEADS))
                if "N" in here:
                    rotate_queries(n, 1)
                    rotate_keys(n)
                if "F" in here:
                    route(f)
                    choose(f)
                if "A" in here:
                    quotient(i, 0)
                    quotient_lo(i, 0)
                if "F" in here:
                    v_low(f)
                if "N" in here:
                    for t in range(TILES):
                        cols = slice(t * P, (t + 1) * P)
                        wait(dve, "qk_hi_ready", n, t + 1)
                        dve.tensor_tensor(q_lo[:, :, cols].bitcast(F32R),
                                          bank("qkT", t)[:, :].rearrange("p (c q) -> p c q", c=CHUNKS),
                                          q_hi[:, :, cols], ALU.subtract).then_inc(S["qk_lo_ready"], 1)
                    wait(dve, "qk_hi_ready", n)
                    dve.tensor_tensor(k_lo.bitcast(F32R), bank("qkT", 2)[:, 0:SEQ], k_hi, ALU.subtract
                                      ).then_inc(S["qk_lo_ready"], 1)
                if "A" in here:
                    quotient(i, 1)
                    quotient_lo(i, 1)
                if "F" in here:
                    spread_v(f, i if "A" in here else None)
                if here == "N":
                    dve.wait_ge(S["gated"], 1)
                    dve.tensor_scalar(gated_bias[:, :], gated_bias[:, :], gates[:, 1:2], None, ALU.mult
                                      ).then_inc(S["gated"], 1)
                    for c in LO_BY_DVE:
                        split_lo(dve, c)
                if "A" in here:
                    residual(i)
                if "F" in here:
                    result(f)

            run(dve, step)

        @block.gpsimd
        def _(pool):
            def step(i, here, before):
                f, n = i - 1, i + 1
                if here == "N":
                    pool.memset(minus_half[:, :], -0.5).then_inc(S["exponents"], 1)
                    pool.wait_ge(S["exponents"], 1)
                if "N" in here:
                    wait(pool, "rms_ready", n)
                    flat = rms[:, :, :].rearrange("p a t -> p (a t)")
                    pool.tensor_tensor(flat, flat, minus_half[:, :], ALU.pow).then_inc(S["rooted"], 1)
                if here == "N":
                    for c in LO_BY_POOL:
                        split_lo(pool, c)
                if "F" in here:
                    wait(pool, "x1_ready", f)
                    wait(pool, "x_out_free", f)
                    pool.wait_ge(S["gated"], 2)
                    pool.tensor_tensor(x_out[:, :, :], x_res[:, :, :],
                                       gated_bias[:, :].unsqueeze(1).broadcast_to([P, TILES, DIM]), ALU.add
                                       ).then_inc(S["biased"], 1)
                if "A" in here:
                    for u in range(8):
                        t, g = u // KV, u % KV
                        block_ = (probs1[:, g, 1, :] if t else probs0[:, g, :]).rearrange("p (n q) -> p n q", n=GROUP)
                        settled_wait(pool, "exp_done", i, 5 + 2 * g if t else g + 1)
                        pool.affine_select(out=block_, in_=block_, compare_op=ALU.is_ge, fill=0.0, base=0,
                                           pattern=[[0, GROUP], [1, P]], channel_multiplier=-1
                                           ).then_inc(S["masked"], 1)
                if "F" in here:
                    wait(pool, "v_lo_ready", f)
                    if "A" in here:
                        wait(pool, "pv_done", i)
                    for k in range(2):
                        js = slice(4 * k, 4 * k + 4)
                        pool.tensor_tensor(u_lo[:, js, :], spread[:, js, :],
                                           v_lo[:, :].bitcast(F32).unsqueeze(1).broadcast_to([P, 4, SEQ]), ALU.mult
                                           ).then_inc(S["u_lo_ready"], 1)
                if "A" in here:
                    for t in range(TILES):
                        wait(pool, "var_ready", i, t + 1)
                        pool.tensor_tensor(r_rms[:, t:t + 1], r_rms[:, t:t + 1], minus_half[:, 0:1], ALU.pow
                                           ).then_inc(S["y_rooted"], 1)

            run(pool, step)


W_PIECES = [("o", 0), ("o", 1), ("a", 0), ("a", 1), ("a", 2), ("a", 3), ("w", 0), ("w", 1),
            ("b", 0), ("b", 1), ("b", 2), ("b", 3)]
PIECE = 1024
LO_BY_POOL, LO_BY_DVE, X_OUT_LAST = (0, 1, 2, 3, 4, 7), (5, 6, 8, 9, 10, 11), 7


def w_part(w, c):
    name, k = W_PIECES[c]
    return w[name][:, :, :].rearrange("p a b -> p (a b)")[:, k * PIECE:(k + 1) * PIECE]


def constants():
    t = np.zeros((P, N_CONST), np.float32)

    def put(name, value):
        t[:, slice(*CONST_COLS[name])] = np.asarray(value, np.float32).reshape(P, -1)

    r = np.arange(P)
    put("ident", np.eye(P))
    put("spread_sum", (r[:, None] % RANK == r[None, :] % RANK) / TOPK ** 2)
    col = np.arange(HD)
    put("pick", np.stack([col[None, :] == parity * PER_CHUNK + r[:, None] // RANK for parity in range(2)], 1))
    k = np.arange(P)
    diagonal = np.where(k[None, :] <= r[:, None], 0.0, NEG)
    put("mask", np.concatenate([np.zeros((P, P)), diagonal], 1))
    inv = (np.float32(1.0) / np.float32(10000.0) ** (np.arange(0, HD, 2, dtype=np.float32) / np.float32(HD)))
    freqs = np.outer(np.arange(SEQ, dtype=np.float32), inv.astype(np.float32)).astype(np.float32)
    cos = np.concatenate([np.cos(freqs), np.cos(freqs)], 1)
    sin = np.concatenate([-np.sin(freqs), np.sin(freqs)], 1)
    put("cos", cos.reshape(TILES, P, HD).transpose(1, 0, 2))
    put("sin", sin.reshape(TILES, P, HD).transpose(1, 0, 2))
    j = np.arange(ROUTES)
    row = HD * (j // 2) + (j % 2) * PER_CHUNK
    put("expand", r[:, None, None] == row[None, :, None] + r[None, None, :] // RANK)
    return t


def kernel(**inputs):
    import concourse.bacc as bacc
    from concourse.bass_utils import run_bass_kernel_spmd

    w_out, A, B, W = (np.asarray(inputs[k]) for k in ("L0_xattn_w_out", "L0_ffn_A", "L0_ffn_B", "L0_ffn_W"))
    o = w_out.reshape(DIM, KV, GROUP, HD).transpose(1, 3, 2, 0).reshape(P, CHUNKS * DIM)
    at = A.reshape(ADAPTERS * RANK, CHUNKS, P).transpose(2, 1, 0).reshape(P, -1)
    wt = W.reshape(DIM, CHUNKS, P).transpose(2, 1, 0).reshape(P, -1)
    bt = B.transpose(0, 2, 1).reshape(ROUTES, P, DIM).transpose(1, 0, 2).reshape(P, -1)
    pieces = np.concatenate([o, at, wt, bt], 1).reshape(P, len(W_PIECES), PIECE).transpose(1, 0, 2)
    given = {
        "x": inputs["x"], "ctx": inputs["ctx_512"], "weights": pieces, "const": constants(),
        "qw": np.asarray(inputs["L0_xattn_q_norm_w"]).reshape(1, DIM),
        "kw": np.asarray(inputs["L0_xattn_k_norm_w"]).reshape(1, CTX),
        "bias": np.asarray(inputs["L0_ffn_bias"]).reshape(1, DIM),
        "g_x": np.asarray(inputs["g_xattn"]).reshape(1, 1), "g_f": np.asarray(inputs["g_ffn"]).reshape(1, 1),
    }
    nc = bacc.Bacc("TRN2", target_bir_lowering=False, num_devices=1)
    arrays, a = {}, {}
    for name, value in given.items():
        value = np.ascontiguousarray(value)
        arrays[f"in_{name}"] = value
        a[name] = nc.dram_tensor(f"in_{name}", value.shape, mybir.dt.from_np(value.dtype), kind="ExternalInput").ap()
    a["out"] = nc.dram_tensor("out_0", (BATCHES, SEQ, DIM), F32, kind="ExternalOutput").ap()
    build(nc, a)
    r = run_bass_kernel_spmd(nc, [arrays], core_ids=[0])
    return r.results[0]["out_0"]
```

```python
import numpy as np

import concourse.bass as bass
from concourse import mybir
from contextlib import ExitStack

F32 = mybir.dt.float32
F32R = mybir.dt.float32r
BF16 = mybir.dt.bfloat16
ALU = mybir.AluOpType
ACT = mybir.ActivationFunctionType
AX = mybir.AxisListType

P = 128
BATCHES, SEQ, DIM = 8, 256, 512
TILES = SEQ // P
HEADS, KV = 16, 4
HD = DIM // HEADS
GROUP = HEADS // KV
CTX = KV * HD
CHUNKS = DIM // P
ADAPTERS, RANK, TOPK = 64, 16, 4
PER_CHUNK = P // RANK
ROUTES = ADAPTERS // PER_CHUNK
EPS = 1e-5
SCALE = HD ** -0.5
NEG = -1e30
LOWEST = -3.0e38
SHIFT_ROW = 3 * HD

CONST_COLS = {}
_at = 0
for _name, _n in (("ident", P), ("spread_sum", P), ("pick", 2 * HD), ("mask", 2 * P), ("cos", TILES * HD),
                  ("sin", TILES * HD), ("expand", ROUTES * P)):
    CONST_COLS[_name] = (_at, _at + _n)
    _at += _n
N_CONST = _at
N_KEPT = CONST_COLS["mask"][1]

BANKS = 6


def _unit_order():
    u = [("F", "yT", 0), ("F", "yT", 1)]
    for v in range(4):
        u += [("A", "scores", 4 * v + k) for k in range(4)] + [("F", "vecs", v)]
    u += [("A", "maxT", 0), ("F", "ssq", 0), ("F", "normT", 0)]
    u += [("A", "st", n) for n in range(4)]
    u += [("F", "maskT", 0)] + [("A", "st", n) for n in range(4, 6)]
    u += [("F", "spread", v) for v in range(4)] + [("A", "st", n) for n in range(6, 12)]
    u += [("A", "pv", 0), ("A", "pv", 1), ("N", "qkT", 0), ("N", "qkT", 1), ("N", "qkT", 2)]
    u += [("A", "pv", 2), ("A", "pv", 3), ("F", "vsum", 0), ("A", "proj", 0), ("A", "proj", 1)]
    return u


UNITS = _unit_order()
PLACE = {(kind, n): at for at, (_, kind, n) in enumerate(UNITS)}


def bank_of(kind, n):
    return PLACE[(kind, n)] % BANKS


def held_before(kind, n, here, before):
    at = PLACE[(kind, n)]
    for k in range(at - 1, -1, -1):
        if k % BANKS == at % BANKS and UNITS[k][0] in here:
            return (*UNITS[k], 0)
    for k in range(len(UNITS) - 1, -1, -1):
        if k % BANKS == at % BANKS and UNITS[k][0] in before:
            return (*UNITS[k], 1)
    return None


def build(nc, a):
    ctx = ExitStack()
    with ctx:
        def sb(name, shape, dt=F32):
            return ctx.enter_context(nc.sbuf_tensor(name, [P, *shape], dt))

        def sem(name):
            return ctx.enter_context(nc.semaphore(name))

        arena = (nc.sbuf_base + 31) // 32 * 32
        probs0 = sb("probs0", [KV, GROUP * P])
        probs1 = sb("probs1", [KV, 2, GROUP * P])
        half = KV * GROUP * P * 4
        o_hi = nc.alloc_sbuf_tensor_at("o_hi", [P, TILES, DIM], F32R, offset=arena)
        o_lo = nc.alloc_sbuf_tensor_at("o_lo", [P, TILES, DIM], F32R, offset=arena + half // 2)
        u_hi = nc.alloc_sbuf_tensor_at("u_hi", [P, ROUTES, SEQ], F32R, offset=arena + half)
        u_lo = nc.alloc_sbuf_tensor_at("u_lo", [P, ROUTES, SEQ], F32R, offset=arena + 2 * half)
        squares = probs1[:, :, :, :].rearrange("p g k c -> p (g k c)")[:, 0:ROUTES * SEQ].rearrange(
            "p (j t) -> p j t", j=ROUTES)
        expand_f = probs1[:, :, :, :].rearrange("p g k c -> p (g k c)")[:, 0:ROUTES * P]

        w_shape = {"o": (CHUNKS, DIM), "a": (CHUNKS, ADAPTERS * RANK), "w": (CHUNKS, DIM), "b": (ROUTES, DIM)}
        w_hi = {k: sb(f"w_{k}_hi", s, F32R) for k, s in w_shape.items()}
        w_lo = {k: sb(f"w_{k}_lo", s, F32R) for k, s in w_shape.items()}

        x_next = sb("x_next", [TILES, DIM])
        x_res = sb("x_res", [TILES, DIM])
        x_out = sb("x_out", [TILES, DIM])
        ctx_next = sb("ctx_next", [TILES, CTX])
        values = sb("values", [TILES, CTX])

        q_cos = sb("q_cos", [TILES, DIM])
        q_sin = sb("q_sin", [TILES, DIM])
        k_cos = sb("k_cos", [TILES, CTX])
        k_sin = sb("k_sin", [TILES, CTX])
        const = sb("const", [N_KEPT])
        ident, spread_sum, pick, mask = (const[:, slice(*CONST_COLS[k])]
                                         for k in ("ident", "spread_sum", "pick", "mask"))
        ident_bf = sb("ident_bf", [P], BF16)
        expand = sb("expand", [ROUTES, P], BF16)
        ones = sb("ones", [HD])
        gated_bias = sb("gated_bias", [DIM])
        gates = sb("gates", [2])
        minus_half = sb("minus_half", [2 * TILES])

        scratch = sb("scratch", [TILES, DIM])
        roped = sb("roped", [TILES, DIM])
        k_norm = sb("k_norm", [TILES, CTX])
        k_rope = sb("k_rope", [TILES, CTX])
        stats = sb("stats", [TILES, 6])
        aggr = sb("aggr", [TILES, 2])
        k_stats = sb("k_stats", [TILES, 6])
        k_aggr = sb("k_aggr", [TILES, 2])
        rms = sb("rms", [2, TILES])
        r_stats = sb("r_stats", [TILES, 6])
        r_aggr = sb("r_aggr", [TILES, 2])
        r_rms = sb("r_rms", [TILES])
        inverse = sb("inverse", [DIM // HD])
        q_stack = sb("q_stack", [HEADS, SEQ], F32R)
        k_stack = sb("k_stack", [KV, SEQ], F32R)
        maxima = sb("maxima", [TILES * HEADS])
        minus_max = sb("minus_max", [P])

        y_arena = (nc.sbuf_base + 31) // 32 * 32
        yT_hi = sb("yT_hi", [CHUNKS, SEQ], F32R)
        yT_lo = sb("yT_lo", [CHUNKS, SEQ], F32R)
        vecs = sb("vecs", [ROUTES, SEQ])
        q_hi, q_lo = vecs[:, 0:CHUNKS, :], vecs[:, CHUNKS:ROUTES, :]
        k_hi, k_lo = roped[:, 0, 0:SEQ], roped[:, 0, SEQ:2 * SEQ]
        spread = sb("spread", [ROUTES, SEQ], BF16)
        ssqT = sb("ssqT", [SEQ])
        norms = sb("norms", [TILES, ADAPTERS + 8])
        top = sb("top", [TILES, 8])
        wanted = sb("wanted", [TILES, 8])
        replaced = sb("replaced", [TILES, ADAPTERS + 8])
        chosen = sb("chosen", [TILES, P], BF16)
        chosenT = sb("chosenT", [SEQ], BF16)
        v_hi = sb("v_hi", [SEQ], F32R)
        v_lo = sb("v_lo", [SEQ], F32R)

        qw_b = vecs[:, 4:6, :].rearrange("p a b -> p (a b)")
        kw_b = vecs[:, 6, 0:CTX]
        trig = ssqT[:, 0:2 * TILES * HD]
        stage = [x_out[:, :, :].rearrange("p a b -> p (a b)"),
                 spread[:, :, :].rearrange("p a b -> p (a b)").bitcast(F32),
                 *(nc.alloc_sbuf_tensor_at(f"in_yT_{k}", [P, PIECE], F32, offset=y_arena + 4 * PIECE * k)[:, :]
                   for k in range(2)),
                 *(probs1[:, g, :, :].rearrange("p k c -> p (k c)") for g in range(1, KV)),
                 x_res[:, :, :].rearrange("p a b -> p (a b)")]

        banks = [ctx.enter_context(nc.psum_tensor(f"bank{k}", [P, 512], F32)) for k in range(BANKS)]
        acc = [ctx.enter_context(nc.psum_tensor(f"acc{t}", [P, 512], F32)) for t in range(TILES)]

        def bank(kind, n):
            return banks[bank_of(kind, n)]

        PER = dict(
            x_loaded=16, ctx_loaded=16, values_loaded=16, res_loaded=16, stacked0=96, stacked1=96, stacked2=96, stacked3=96, shift_stacked=32,
            x_out_free=32,
            yT_done=2, scores_done=16, vecs_done=4, ssq_done=1, maxT_done=1, normT_done=1, st_done=12,
            maskT_done=1, spread_done=4, pv_done=4, vsum_done=1, qkT_done=3, proj_done=2, acc_done=2,
            yT_hi_ready=2, vecs_ready=4, squared=4, ssqT_ready=1, minus_ready=1, exp_done=12, chosenT_ready=1,
            spread_ready=4, o_hi_ready=2, v_hi_ready=1, qk_hi_ready=3,
            yT_lo_ready=2, maxed=32, norms_taken=1, routed=1, stat_step=10, q_step=8, k_step=5, q_roped=2, k_roped=1, picked=4,
            vsum_ready=1, sums_taken=2, norm_step=4, quotient_ready=2, o_lo_ready=2, v_lo_ready=1, u_hi_ready=2, qk_lo_ready=3,
            x1_ready=2, y_step=4, rms_ready=1, var_ready=2, y_ready=2, out_ready=2, route_step=5,
            biased=1, masked=8, rooted=1, y_rooted=2, u_lo_ready=2)
        ONCE = ("const_loaded", "trig_loaded", "expand_loaded", "vectors_loaded", "gates_loaded", "w_hi_done",
                "w_lo_by_pool", "w_lo_by_dve", *(f"w{s}_loaded" for s in range(len(stage))), "tables", "gated", "constants", "expand_ready", "fills", "exponents")
        S = {k: sem(k) for k in (*PER, *ONCE)}

        def wait(eng, name, batch, done=None):
            eng.wait_ge(S[name], PER[name] * batch + (PER[name] if done is None else done))

        def settled_wait(eng, name, batch, done=None):
            value = PER[name] * batch + (PER[name] if done is None else done)
            if not isinstance(batch, int):
                value = eng.compute_val(value)
                eng.wait_ge(S[name], 1)
            eng.wait_ge(S[name], value)

        def split_lo(eng, c):
            s = c % len(stage)
            eng.wait_ge(S["w_hi_done"], c + 1)
            ins = eng.tensor_tensor(w_part(w_lo, c), stage[s], w_part(w_hi, c).bitcast(F32), ALU.subtract)
            if c == X_OUT_LAST:
                ins.then_inc(S["x_out_free"], 32)
            else:
                ins.then_inc(S["w_lo_by_pool" if c in LO_BY_POOL else "w_lo_by_dve"], 1)

        def wait_split(eng, c):
            if c == X_OUT_LAST:
                eng.wait_ge(S["x_out_free"], 32)
            elif c in LO_BY_POOL:
                eng.wait_ge(S["w_lo_by_pool"], LO_BY_POOL.index(c) + 1)
            else:
                eng.wait_ge(S["w_lo_by_dve"], LO_BY_DVE.index(c) + 1)

        def wait_all_split(eng):
            eng.wait_ge(S["x_out_free"], 32)
            eng.wait_ge(S["w_lo_by_pool"], len(LO_BY_POOL) - 1)
            eng.wait_ge(S["w_lo_by_dve"], len(LO_BY_DVE))

        READ = {"yT": lambda n: ("yT_lo_ready", n + 1), "scores": lambda n: ("maxed", 2 * n + 2),
                "vecs": lambda n: ("vecs_ready", n + 1), "ssq": lambda n: ("ssqT_ready", 1),
                "maxT": lambda n: ("minus_ready", 1), "normT": lambda n: ("norms_taken", 1),
                "st": lambda n: ("exp_done", n + 1), "maskT": lambda n: ("chosenT_ready", 1),
                "spread": lambda n: ("spread_ready", n + 1),
                "pv": lambda n: (("sums_taken", "quotient_ready")[n % 2], n // 2 + 1),
                "vsum": lambda n: ("v_lo_ready", 1), "qkT": lambda n: ("qk_lo_ready", n + 1),
                "proj": lambda n: ("x1_ready", n + 1)}
        AHEAD = {"A": 0, "F": -1, "N": 1}

        def heads_of(u):
            g, t, pair = u // 4, u // 2 % 2, u % 2
            return (GROUP * g + 2 * pair, GROUP * g + 2 * pair + 1), t

        def tile_of(u):
            return (u, 0, 0) if u < KV else ((u - KV) // 2, 1 - (u - KV) % 2, 1)

        def chain(eng, name, batch):
            count = [0]

            def did(ins, last=False):
                count[0] += 1
                assert count[0] <= PER[name]
                ins.then_inc(S[name], 1)

            def settle():
                wait(eng, name, batch, count[0])
            return did, settle

        def halves(ap, s):
            return ap.rearrange("p (g n s d) -> p g n s d", g=KV, s=2, d=HD // 2)[:, :, :, s, :]

        def run(eng, step):
            step(-1, "NX", "")
            step(0, "ANX", "N")
            with eng.Fori(1, BATCHES - 2) as i:
                step(i, "FANX", "AN")
            step(BATCHES - 2, "FAN", "FAN")
            step(BATCHES - 1, "FA", "FAN")
            step(BATCHES, "F", "FA")

        block = ctx.enter_context(nc.Block())

        @block.sync
        def _(sp):
            def load_values(b):
                sp.dma_start(values[:, :, :], a["ctx"][b].rearrange("(t p) c -> p t c", p=P)
                             ).then_inc(S["values_loaded"], 16)

            def load_res(b):
                sp.dma_start(x_res[:, :, :], a["x"][b].rearrange("(t p) c -> p t c", p=P)
                             ).then_inc(S["res_loaded"], 16)

            def step(i, here, before):
                if here == "NX":
                    sp.dma_start(trig, a["const"][:, CONST_COLS["cos"][0]:CONST_COLS["sin"][1]]
                                 ).then_inc(S["trig_loaded"], 16)
                    sp.dma_start(qw_b, a["qw"].broadcast_to([P, DIM])).then_inc(S["vectors_loaded"], 16)
                    sp.dma_start(kw_b, a["kw"].broadcast_to([P, CTX])).then_inc(S["vectors_loaded"], 16)
                    sp.dma_start(const[:, :], a["const"][:, 0:N_KEPT]).then_inc(S["const_loaded"], 16)
                    sp.dma_start(gates[:, 0:1], a["g_x"].broadcast_to([P, 1])).then_inc(S["gates_loaded"], 16)
                    sp.dma_start(gates[:, 1:2], a["g_f"].broadcast_to([P, 1])).then_inc(S["gates_loaded"], 16)
                    sp.dma_start(gated_bias[:, :], a["bias"].broadcast_to([P, DIM])).then_inc(S["gates_loaded"], 16)
                    sp.dma_start(expand_f, a["const"][:, slice(*CONST_COLS["expand"])]
                                 ).then_inc(S["expand_loaded"], 16)
                if "A" in here:
                    if "A" in before:
                        wait(sp, "pv_done", i - 1)
                    load_values(i)
                    if "F" in here:
                        wait(sp, "biased", i - 1)
                        wait(sp, "y_ready", i - 1)
                    if here != "ANX":
                        load_res(i)
                    wait(sp, "minus_ready", i)
                    for t in range(TILES):
                        sp.dma_start(q_stack[SHIFT_ROW:SHIFT_ROW + 1, :, t * P:(t + 1) * P].bitcast(F32),
                                     minus_max[t * HEADS:(t + 1) * HEADS, :]).then_inc(S["shift_stacked"], 16)
                    if here == "ANX":
                        wait_split(sp, 7)
                        load_res(i)
                if "N" in here:
                    wait(sp, "qk_lo_ready", i + 1)
                    for g in range(KV):
                        rows = slice(g * HD, (g + 1) * HD)
                        for part, (qs, ks) in enumerate(((q_hi, k_hi), (q_lo, k_hi), (q_hi, k_lo))):
                            to = slice(part * HD, (part + 1) * HD)
                            sp.dma_start(q_stack[to, g * GROUP:(g + 1) * GROUP, :].bitcast(F32), qs[rows]
                                         ).then_inc(S[f"stacked{g}"], 16)
                            sp.dma_start(k_stack[to, g, :].bitcast(F32), ks[rows]).then_inc(S[f"stacked{g}"], 16)
                if "F" in here:
                    for t in range(TILES):
                        wait(sp, "out_ready", i - 1, t + 1)
                        sp.dma_start(a["out"][i - 1][t * P:(t + 1) * P, :], x_out[:, t, :]
                                     ).then_inc(S["x_out_free"], 16)

            run(sp, step)
            wait(sp, "x_out_free", BATCHES)

        @block.tensor
        def _(pe):
            def step(i, here, before):
                def take(kind, n, implied=None):
                    held = held_before(kind, n, here, before)
                    if held:
                        stage_, k, m, ago = held
                        name, count = READ[k](m)
                        if name != implied:
                            wait(pe, name, i + AHEAD[stage_] - ago, count)
                    return bank(kind, n)

                def products(out, terms, name, first=True, last=True):
                    for k, (l, r) in enumerate(terms):
                        ins = nc.tensor.matmul(out, l, r, start=(first and k == 0),
                                               stop=(last and k == len(terms) - 1), skip_group_check=True)
                    if name:
                        ins.then_inc(S[name], 1)

                f, n = i - 1, i + 1

                def y_transposed(t):
                    wait(pe, "y_ready", f, t + 1)
                    ps = take("yT", t)
                    for c in range(CHUNKS):
                        ins = nc.tensor.transpose(ps[:, c * P:(c + 1) * P], scratch[:, t, c * P:(c + 1) * P], ident)
                    ins.then_inc(S["yT_done"], 1)

                def scores(u):
                    heads, t = heads_of(u)
                    if u % GROUP == 0:
                        wait(pe, f"stacked{heads[0] // GROUP}", i)
                    ps = take("scores", u)
                    for k, h in enumerate(heads):
                        ins = nc.tensor.matmul(ps[:, k * SEQ:(k + 1) * SEQ],
                                               q_stack[0:SHIFT_ROW, h, t * P:(t + 1) * P],
                                               k_stack[0:SHIFT_ROW, h // GROUP, :], start=True, stop=True)
                    ins.then_inc(S["scores_done"], 1)

                def adapter_vecs(v):
                    if v == 0:
                        wait(pe, "yT_hi_ready", f)
                    ps = take("vecs", v)
                    for k in range(2):
                        cols = slice((2 * v + k) * P, (2 * v + k + 1) * P)
                        terms = [(w[:, c, cols], y[:, c, :]) for w, y in
                                 ((w_hi["a"], yT_hi), (w_lo["a"], yT_hi), (w_hi["a"], yT_lo)) for c in range(CHUNKS)]
                        out = ps[:, k * SEQ:(k + 1) * SEQ]
                        products(out, terms[:2 * CHUNKS], None, last=False)
                        if v == 0 and k == 0:
                            wait(pe, "yT_lo_ready", f)
                        products(out, terms[2 * CHUNKS:], "vecs_done" if k else None, first=False)

                def squared_norms():
                    wait(pe, "squared", f)
                    ps = take("ssq", 0)
                    for parity in range(2):
                        for q in range(4):
                            ins = nc.tensor.matmul(ps[q * HD:(q + 1) * HD, 0:SEQ],
                                                   pick[:, parity * HD:(parity + 1) * HD],
                                                   squares[:, 2 * q + parity, :], start=(parity == 0),
                                                   stop=(parity == 1), skip_group_check=True)
                    ins.then_inc(S["ssq_done"], 1)

                def norms_transposed():
                    wait(pe, "ssqT_ready", f)
                    ps = take("normT", 0)
                    for t in range(TILES):
                        ins = nc.tensor.transpose(ps[:, t * P:(t + 1) * P], ssqT[:, t * P:(t + 1) * P], ident)
                    ins.then_inc(S["normT_done"], 1)

                def maxima_transposed():
                    wait(pe, "maxed", i)
                    ps = take("maxT", 0)
                    nc.tensor.transpose(ps[0:TILES * HEADS, 0:P], maxima[:, :], ident).then_inc(S["maxT_done"], 1)

                def base(t, start, end):
                    if start == end:
                        return
                    toks = slice(t * P, (t + 1) * P)
                    terms = [(y[:, c, toks], w[:, c, :]) for y, w in
                             ((yT_hi, w_hi["w"]), (yT_lo, w_hi["w"]), (yT_hi, w_lo["w"])) for c in range(CHUNKS)]
                    products(acc[t][:, :], terms[start:end], None, first=(start == 0), last=False)

                def scores_T(u):
                    if u == 0:
                        wait(pe, "shift_stacked", i)
                    ps = take("st", u)
                    g, kb, t = tile_of(u)
                    nc.tensor.matmul(ps[:, :], k_stack[0:SHIFT_ROW + 1, g, kb * P:(kb + 1) * P],
                                     q_stack[0:SHIFT_ROW + 1, g * GROUP:(g + 1) * GROUP, t * P:(t + 1) * P],
                                     start=True, stop=True).then_inc(S["st_done"], 1)

                def mask_transposed():
                    wait(pe, "routed", f)
                    ps = take("maskT", 0)[:, :].bitcast(BF16)
                    for t in range(TILES):
                        ins = nc.tensor.transpose(ps[:, t * P:(t + 1) * P], chosen[:, t, :], ident_bf[:, :])
                    ins.then_inc(S["maskT_done"], 1)

                def mask_spread(v):
                    if v == 0:
                        wait(pe, "chosenT_ready", f)
                    ps = take("spread", v)
                    for k in range(2):
                        ins = nc.tensor.matmul(ps[:, k * SEQ:(k + 1) * SEQ], expand[:, 2 * v + k, :], chosenT[:, :],
                                               start=True, stop=True)
                    ins.then_inc(S["spread_done"], 1)

                def attend(u):
                    t, with_values = u // 2, u % 2
                    if u == 0:
                        wait(pe, "values_loaded", i)
                    if not with_values:
                        wait(pe, "masked", i, 4 * (t + 1))
                        wait(pe, "exp_done", i, (4, 12)[t])
                    ps = take("pv", u)
                    for kb in range(t + 1):
                        for g in range(KV):
                            pr = probs1[:, g, kb, :] if t else probs0[:, g, :]
                            l = values[:, kb, g * HD:(g + 1) * HD] if with_values else ones[:, :]
                            ins = nc.tensor.matmul(ps[g * HD:(g + 1) * HD, :], l, pr, start=(kb == 0),
                                                   stop=(kb == t), skip_group_check=True)
                    ins.then_inc(S["pv_done"], 1)

                def chosen_sum():
                    wait(pe, "vsum_ready", f)
                    ps = take("vsum", 0)
                    nc.tensor.matmul(ps[:, 0:SEQ], spread_sum, ssqT[:, :], start=True, stop=True
                                     ).then_inc(S["vsum_done"], 1)

                def qk_transposed(u):
                    if u < TILES:
                        wait(pe, "q_roped", n, u + 1)
                    else:
                        wait(pe, "k_roped", n)
                    ps = take("qkT", u)
                    for c in range(CHUNKS if u < TILES else TILES):
                        src = roped[:, u, c * P:(c + 1) * P] if u < TILES else k_rope[:, c, :]
                        ins = nc.tensor.transpose(ps[:, c * P:(c + 1) * P], src, ident)
                    ins.then_inc(S["qkT_done"], 1)

                def project(t):
                    wait(pe, "o_hi_ready", i, t + 1)
                    ps = take("proj", t)
                    terms = [(o[:, t, c * P:(c + 1) * P], w[:, c, :]) for o, w in
                             ((o_hi, w_hi["o"]), (o_hi, w_lo["o"]), (o_lo, w_hi["o"])) for c in range(CHUNKS)]
                    products(ps[:, :], terms[:2 * CHUNKS], None, last=False)
                    wait(pe, "o_lo_ready", i, t + 1)
                    products(ps[:, :], terms[2 * CHUNKS:], "proj_done", first=False)

                def delta(t):
                    toks = slice(t * P, (t + 1) * P)
                    for k in range(2):
                        if t == 0:
                            wait(pe, "u_hi_ready", f, k + 1)
                        products(acc[t][:, :], [(u_hi[:, j, toks], w[:, j, :]) for w in (w_hi["b"], w_lo["b"])
                                                for j in range(4 * k, 4 * k + 4)], None, first=False, last=False)
                    if t == 0:
                        wait(pe, "u_lo_ready", f)
                    products(acc[t][:, :], [(u_lo[:, j, toks], w_hi["b"][:, j, :]) for j in range(ROUTES)],
                             "acc_done", first=False)

                if here == "NX":
                    pe.wait_ge(S["const_loaded"], 16)
                    pe.wait_ge(S["constants"], 1)
                    pe.wait_ge(S["fills"], 5)
                F, A, N = "F" in here, "A" in here, "N" in here
                if F:
                    y_transposed(0)
                    y_transposed(1)
                for v in range(4):
                    if A:
                        for k in range(4):
                            scores(4 * v + k)
                    if F:
                        adapter_vecs(v)
                if F:
                    base(0, 0, 4)
                if A:
                    maxima_transposed()
                if F:
                    squared_norms()
                    base(0, 4, 12 if A else 6)
                    norms_transposed()
                    base(0, 12 if A else 6, 12)
                    base(1, 0, 3)
                if A:
                    for u in range(4):
                        scores_T(u)
                if F:
                    base(1, 3, 5 if A else 3)
                    mask_transposed()
                if A:
                    for u in range(4, 6):
                        scores_T(u)
                if F:
                    base(1, 5 if A else 3, 9 if A else 5)
                    for v in range(4):
                        mask_spread(v)
                    base(1, 9 if A else 5, 12)
                if A:
                    for u in range(6, 12):
                        scores_T(u)
                if N and not F:
                    for u in range(3):
                        qk_transposed(u)
                if A:
                    attend(0)
                    attend(1)
                if N and F:
                    for u in range(3):
                        qk_transposed(u)
                if A:
                    attend(2)
                    attend(3)
                if F:
                    chosen_sum()
                if A:
                    if here == "ANX":
                        wait_split(pe, 1)
                    project(0)
                    project(1)
                if here == "ANX":
                    wait_all_split(pe)
                    pe.wait_ge(S["expand_ready"], 1)
                if F:
                    delta(0)
                    delta(1)

            run(pe, step)

        @block.scalar
        def _(act):
            def load_x(n):
                nc.scalar.dma_start(x_next[:, :, :], a["x"][n].rearrange("(t p) c -> p t c", p=P)
                                    ).then_inc(S["x_loaded"], 16)
                nc.scalar.dma_start(ctx_next[:, :, :], a["ctx"][n].rearrange("(t p) c -> p t c", p=P)
                                    ).then_inc(S["ctx_loaded"], 16)

            def load_weights(c):
                s = c % len(stage)
                if c >= len(stage):
                    wait_split(act, c - len(stage))
                nc.scalar.dma_start(stage[s], a["weights"][c]).then_inc(S[f"w{s}_loaded"], 16)

            def split_hi(c):
                act.wait_ge(S[f"w{c % len(stage)}_loaded"], 16 * (c // len(stage) + 1))
                nc.scalar.copy(w_part(w_hi, c), stage[c % len(stage)]).then_inc(S["w_hi_done"], 1)

            def step(i, here, before):
                f, n = i - 1, i + 1

                def exponentials(u):
                    g, kb, t = tile_of(u)
                    to = probs1[:, g, kb, :] if t else probs0[:, g, :]
                    wait(act, "st_done", i, u + 1)
                    nc.scalar.activation(to, bank("st", u)[:, :], ACT.Exp).then_inc(S["exp_done"], 1)

                def quotient_hi(t):
                    wait(act, "quotient_ready", i, t + 1)
                    nc.scalar.copy(o_hi[:, t, :], scratch[:, 1, :]).then_inc(S["o_hi_ready"], 1)

                if here == "NX":
                    load_x(0)
                    act.wait_ge(S["const_loaded"], 16)
                    for c in range(len(stage)):
                        load_weights(c)
                    for c in range(3):
                        split_hi(c)
                if here == "ANX":
                    act.wait_ge(S["expand_loaded"], 16)
                    nc.scalar.copy(expand[:, :, :].rearrange("p j c -> p (j c)"), expand_f
                                   ).then_inc(S["expand_ready"], 1)
                    act.wait_ge(S["gates_loaded"], 48)
                    nc.scalar.activation(gates[:, :], gates[:, :], ACT.Tanh).then_inc(S["gated"], 1)
                    for c in range(3, len(stage)):
                        split_hi(c)
                    wait(act, "stacked3", i)
                    for c in range(len(stage), len(W_PIECES)):
                        load_weights(c)
                if "F" in here:
                    for t in range(TILES):
                        wait(act, "yT_done", f, t + 1)
                        nc.scalar.copy(yT_hi[:, :, t * P:(t + 1) * P],
                                       bank("yT", t)[:, :].rearrange("p (c q) -> p c q", c=CHUNKS)
                                       ).then_inc(S["yT_hi_ready"], 1)
                    for v in range(4):
                        ps = bank("vecs", v)[:, :].rearrange("p (k t) -> p k t", k=2)
                        wait(act, "vecs_done", f, v + 1)
                        nc.scalar.activation(squares[:, 2 * v:2 * v + 2, :], ps, ACT.Square).then_inc(S["squared"], 1)
                        if v == 0 and "A" in here:
                            for g in range(KV):
                                wait(act, f"stacked{g}", i)
                        nc.scalar.copy(vecs[:, 2 * v:2 * v + 2, :], ps).then_inc(S["vecs_ready"], 1)
                if "A" in here:
                    wait(act, "maxT_done", i)
                    nc.scalar.mul(minus_max[0:TILES * HEADS, :].bitcast(F32R), bank("maxT", 0)[0:TILES * HEADS, 0:P],
                                  -1.0).then_inc(S["minus_ready"], 1)
                if here == "ANX":
                    for c in range(len(stage), len(W_PIECES) - 1):
                        split_hi(c)
                if "F" in here:
                    wait(act, "ssq_done", f)
                    nc.scalar.copy(ssqT[:, :], bank("ssq", 0)[:, 0:SEQ]).then_inc(S["ssqT_ready"], 1)
                if "A" in here:
                    for u in range(4):
                        exponentials(u)
                if "F" in here:
                    wait(act, "maskT_done", f)
                    nc.scalar.copy(chosenT[:, :], bank("maskT", 0)[:, :].bitcast(BF16)[:, 0:SEQ]
                                   ).then_inc(S["chosenT_ready"], 1)
                if here == "ANX":
                    for c in (4, 5, 6):
                        wait_split(act, c)
                if "A" in here:
                    for u in range(4, 6):
                        exponentials(u)
                if "F" in here:
                    for v in range(4):
                        wait(act, "spread_done", f, v + 1)
                        nc.scalar.copy(spread[:, 2 * v:2 * v + 2, :],
                                       bank("spread", v)[:, :].rearrange("p (k t) -> p k t", k=2)
                                       ).then_inc(S["spread_ready"], 1)
                if "A" in here:
                    for u in range(6, 12):
                        exponentials(u)
                if here == "ANX":
                    split_hi(len(W_PIECES) - 1)
                if "N" in here:
                    for t in range(TILES):
                        wait(act, "qkT_done", n, t + 1)
                        if t == 0 and "F" in here:
                            wait(act, "vsum_ready", f)
                        nc.scalar.copy(q_hi[:, :, t * P:(t + 1) * P].bitcast(F32R),
                                       bank("qkT", t)[:, :].rearrange("p (c q) -> p c q", c=CHUNKS)
                                       ).then_inc(S["qk_hi_ready"], 1)
                    wait(act, "qkT_done", n)
                    nc.scalar.copy(k_hi.bitcast(F32R), bank("qkT", 2)[:, 0:SEQ]).then_inc(S["qk_hi_ready"], 1)
                if "A" in here:
                    quotient_hi(0)
                if "F" in here:
                    wait(act, "vsum_done", f)
                    nc.scalar.copy(v_hi[:, :], bank("vsum", 0)[:, 0:SEQ]).then_inc(S["v_hi_ready"], 1)
                if "X" in here:
                    wait(act, "k_roped", n)
                    load_x(n + 1)
                if "A" in here:
                    quotient_hi(1)

            run(act, step)

        @block.vector
        def _(dve):
            def tables():
                cos, sin = (trig[:, k * TILES * HD:(k + 1) * TILES * HD] for k in range(2))
                todo = []
                for heads, w, to_cos, to_sin in ((HEADS, qw_b, q_cos, q_sin), (KV, kw_b, k_cos, k_sin)):
                    hd = HD // 2
                    for t in range(TILES):
                        at = lambda ap, s: ap.rearrange("p (h s d) -> p h s d", h=heads, s=2)[:, :, s, :]
                        wide = lambda ap, s: ap[:, t * HD + s * hd:t * HD + (s + 1) * hd].unsqueeze(1).broadcast_to(
                            [P, heads, hd])
                        for s in range(2):
                            todo.append((at(to_cos[:, t, :], s), at(w, s), wide(cos, s)))
                            todo.append((at(to_sin[:, t, :], s), at(w, 1 - s), wide(sin, s)))
                for out, l, r in todo:
                    dve.tensor_tensor(out, l, r, ALU.mult).then_inc(S["tables"], 1)
                return len(todo)

            def statistics(n):
                did, settle = chain(dve, "stat_step", n)
                wait(dve, "x_loaded", n)
                for t in range(TILES):
                    did(dve.bn_stats(stats[:, t, :], x_next[:, t, :]))
                wait(dve, "ctx_loaded", n)
                for t in range(TILES):
                    did(dve.bn_stats(k_stats[:, t, :], ctx_next[:, t, :]))
                settled_wait(dve, "stat_step", n, 4)
                for t in range(TILES):
                    did(dve.bn_aggr(aggr[:, t, :], stats[:, t, :]))
                    did(dve.bn_aggr(k_aggr[:, t, :], k_stats[:, t, :]))
                settle()
                did(dve.tensor_scalar(rms[:, 0, :], aggr[:, :, 1], HD * (1.0 + EPS), HD * EPS * EPS,
                                      ALU.mult, ALU.add))
                did(dve.tensor_tensor(rms[:, 1, :], k_aggr[:, :, 0], k_aggr[:, :, 0], ALU.mult))
                settle()
                dve.scalar_tensor_tensor(out=rms[:, 1, :], in0=k_aggr[:, :, 1], scalar=EPS, in1=rms[:, 1, :],
                                         op0=ALU.add, op1=ALU.add).then_inc(S["rms_ready"], 1)

            normed, product = scratch[:, 0, :], scratch[:, 1, :]

            def rotate_queries(n, t, part, after):
                out = roped[:, t, :].rearrange("p (n g d) -> p g n d", n=GROUP, g=KV)
                heads = lambda ap: ap.rearrange("p (g n d) -> p g n d", g=KV, n=GROUP)
                if part == 0:
                    if t == 0:
                        wait(dve, "rooted", n)
                    dve.tensor_scalar(normed, x_next[:, t, :], aggr[:, t, 0:1], rms[:, 0, t:t + 1],
                                      ALU.subtract, ALU.mult).then_inc(S["q_step"], 1)
                    wait(dve, "q_step", n, 4 * t + 1)
                    for s in range(2):
                        dve.tensor_tensor(halves(product, s), halves(normed, 1 - s), halves(q_sin[:, t, :], s),
                                          ALU.mult).then_inc(S["q_step"], 1)
                else:
                    if t == 0 and after:
                        for g in range(KV):
                            wait(dve, f"stacked{g}", n - 1)
                    dve.tensor_tensor(out, heads(normed), heads(q_cos[:, t, :]), ALU.mult).then_inc(S["q_step"], 1)
                    wait(dve, "q_step", n, 4 * t + 4)
                    dve.tensor_tensor(out, out, heads(product), ALU.add).then_inc(S["q_roped"], 1)

            def rotate_keys(n):
                did, settle = chain(dve, "k_step", n)
                for t in range(TILES):
                    did(dve.tensor_scalar(k_norm[:, t, :], ctx_next[:, t, :], rms[:, 1, t:t + 1], None, ALU.mult))
                settle()
                flat = lambda ap: ap[:, :, :].rearrange("p t c -> p (t c)")
                swap = lambda ap, s: ap.rearrange("p (h s d) -> p h s d", s=2, d=HD // 2)[:, :, s, :]
                did(dve.tensor_tensor(flat(k_rope), flat(k_norm), flat(k_cos), ALU.mult))
                wait(dve, "q_roped", n)
                for s in range(2):
                    did(dve.tensor_tensor(swap(product[:, 0:TILES * CTX], s), swap(flat(k_norm), 1 - s),
                                          swap(flat(k_sin), s), ALU.mult))
                settle()
                dve.tensor_tensor(flat(k_rope), flat(k_rope), product[:, 0:TILES * CTX], ALU.add
                                  ).then_inc(S["k_roped"], 1)

            def maxima_of(b, units):
                for u in units:
                    (heads, t), ps = heads_of(u), bank("scores", u)
                    settled_wait(dve, "scores_done", b, u + 1)
                    if u >= 4:
                        settled_wait(dve, "maxed", b, 2 * u - 6)
                    for k, h in enumerate(heads):
                        keys = (t + 1) * P
                        slot = probs0[:, u % 4, k * SEQ:k * SEQ + keys]
                        dve.tensor_tensor_reduce(slot, ps[:, k * SEQ:k * SEQ + keys],
                                                 mask[:, 2 * P - keys:2 * P], 1.0, LOWEST, ALU.add, ALU.max,
                                                 maxima[:, t * HEADS + h:t * HEADS + h + 1]).then_inc(S["maxed"], 1)

            def route(f):
                did, settle = chain(dve, "route_step", f)
                wait(dve, "normT_done", f)
                dve.tensor_copy(norms[:, :, 0:ADAPTERS].rearrange("p t (q a) -> p t q a", q=4),
                                bank("normT", 0)[:, 0:TILES * P].rearrange("p (t q a) -> p t q a", t=TILES, q=4
                                                                          )[:, :, :, 0:RANK]
                                ).then_inc(S["norms_taken"], 1)
                settled_wait(dve, "norms_taken", f)
                for t in range(TILES):
                    did(dve.max(top[:, t, :], norms[:, t, 0:ADAPTERS]))
                settle()
                did(dve.tensor_copy(wanted[:, :, 0:TOPK], top[:, :, 0:TOPK]))
                settled_wait(dve, "route_step", f, 3)
                for t in range(TILES):
                    did(dve.match_replace(replaced[:, t, :], wanted[:, t, :], norms[:, t, :], -2.0))
                settle()
                dve.tensor_scalar(chosen[:, :, :].rearrange("p t (q a) -> p t q a", q=4)[:, :, :, 0:RANK],
                                  replaced[:, :, 0:ADAPTERS].rearrange("p t (q a) -> p t q a", q=4),
                                  -1.5, None, ALU.is_lt).then_inc(S["routed"], 1)

            def choose(f):
                for v in range(4):
                    wait(dve, "spread_ready", f, v + 1)
                    if v == 0:
                        wait(dve, "vecs_ready", f)
                    part = vecs[:, 2 * v:2 * v + 2, :]
                    dve.tensor_tensor(part, part, spread[:, 2 * v:2 * v + 2, :], ALU.mult).then_inc(S["picked"], 1)
                wait(dve, "picked", f)
                dve.tensor_reduce(ssqT[:, :], vecs[:, :, :].rearrange("p j t -> p t j"), AX.X, ALU.add
                                  ).then_inc(S["vsum_ready"], 1)

            sums = scratch[:, 0, :]

            def inverse_sums(b, t):
                wait(dve, "pv_done", b, 2 * t + 1)
                dve.transpose(sums, bank("pv", 2 * t)[:, :]).then_inc(S["sums_taken"], 1)
                wait(dve, "sums_taken", b, t + 1)
                dve.reciprocal(inverse[:, :], sums.rearrange("p (k r) -> p k r", r=HD)[:, :, 0]
                               ).then_inc(S["norm_step"], 1)
                wait(dve, "norm_step", b, 2 * t + 1)
                dve.transpose(sums, inverse[:, :].unsqueeze(2).broadcast_to([P, DIM // HD, HD])
                              ).then_inc(S["norm_step"], 1)

            def quotient(b, t):
                wait(dve, "norm_step", b, 2 * t + 2)
                wait(dve, "pv_done", b, 2 * t + 2)
                if t:
                    wait(dve, "o_hi_ready", b, t)
                dve.tensor_tensor(scratch[:, 1, :], bank("pv", 2 * t + 1)[:, :], sums, ALU.mult
                                  ).then_inc(S["quotient_ready"], 1)

            def quotient_lo(b, t):
                wait(dve, "o_hi_ready", b, t + 1)
                dve.tensor_tensor(o_lo[:, t, :], scratch[:, 1, :], o_hi[:, t, :].bitcast(F32), ALU.subtract
                                  ).then_inc(S["o_lo_ready"], 1)

            def v_low(f):
                wait(dve, "v_hi_ready", f)
                dve.tensor_tensor(v_lo[:, :], bank("vsum", 0)[:, 0:SEQ], v_hi[:, :].bitcast(F32), ALU.subtract
                                  ).then_inc(S["v_lo_ready"], 1)

            def spread_v(f, b):
                if b is not None:
                    wait(dve, "pv_done", b)
                for k in range(2):
                    js = slice(4 * k, 4 * k + 4)
                    dve.tensor_tensor(u_hi[:, js, :], spread[:, js, :],
                                      v_hi[:, :].bitcast(F32).unsqueeze(1).broadcast_to([P, 4, SEQ]), ALU.mult
                                      ).then_inc(S["u_hi_ready"], 1)

            def low_queries(n, t):
                cols = slice(t * P, (t + 1) * P)
                wait(dve, "qk_hi_ready", n, t + 1)
                dve.tensor_tensor(q_lo[:, :, cols].bitcast(F32R),
                                  bank("qkT", t)[:, :].rearrange("p (c q) -> p c q", c=CHUNKS),
                                  q_hi[:, :, cols], ALU.subtract).then_inc(S["qk_lo_ready"], 1)

            def low_keys(n):
                wait(dve, "qk_hi_ready", n)
                dve.tensor_tensor(k_lo.bitcast(F32R), bank("qkT", 2)[:, 0:SEQ], k_hi, ALU.subtract
                                  ).then_inc(S["qk_lo_ready"], 1)

            def residual(b):
                did, settle = chain(dve, "y_step", b)
                for t in range(TILES):
                    wait(dve, "proj_done", b, t + 1)
                    if t == 0:
                        wait(dve, "res_loaded", b)
                    dve.scalar_tensor_tensor(out=x_res[:, t, :], in0=bank("proj", t)[:, :], scalar=gates[:, 0:1],
                                             in1=x_res[:, t, :], op0=ALU.mult, op1=ALU.add
                                             ).then_inc(S["x1_ready"], 1)
                    wait(dve, "x1_ready", b, t + 1)
                    did(dve.bn_stats(r_stats[:, t, :], x_res[:, t, :]))
                    settled_wait(dve, "y_step", b, 2 * t + 1)
                    did(dve.bn_aggr(r_aggr[:, t, :], r_stats[:, t, :]))
                    settle()
                    dve.tensor_scalar(r_rms[:, t:t + 1], r_aggr[:, t, 1:2], EPS, None, ALU.add
                                      ).then_inc(S["var_ready"], 1)
                    wait(dve, "y_rooted", b, t + 1)
                    dve.tensor_scalar(scratch[:, t, :], x_res[:, t, :], r_aggr[:, t, 0:1], r_rms[:, t:t + 1],
                                      ALU.subtract, ALU.mult).then_inc(S["y_ready"], 1)

            def result(f):
                wait(dve, "biased", f)
                for t in range(TILES):
                    wait(dve, "acc_done", f, t + 1)
                    dve.scalar_tensor_tensor(out=x_out[:, t, :], in0=acc[t][:, :], scalar=gates[:, 1:2],
                                             in1=x_out[:, t, :], op0=ALU.mult, op1=ALU.add
                                             ).then_inc(S["out_ready"], 1)

            def step(i, here, before):
                f, n = i - 1, i + 1
                if here == "NX":
                    dve.memset(ones[:, :], 1.0).then_inc(S["fills"], 1)
                    dve.memset(k_stack[SHIFT_ROW:SHIFT_ROW + 1, :, :].bitcast(F32), 1.0).then_inc(S["fills"], 1)
                    dve.memset(norms[:, :, ADAPTERS:], -1.0).then_inc(S["fills"], 1)
                    dve.memset(wanted[:, :, :], -1.0).then_inc(S["fills"], 1)
                    dve.memset(chosen[:, :, :], 0.0).then_inc(S["fills"], 1)
                    dve.wait_ge(S["fills"], 5)
                    statistics(n)
                    dve.wait_ge(S["trig_loaded"], 16)
                    dve.wait_ge(S["vectors_loaded"], 32)
                    dve.wait_ge(S["tables"], tables())
                    dve.wait_ge(S["const_loaded"], 16)
                    dve.tensor_copy(ident_bf[:, :], ident).then_inc(S["constants"], 1)
                if "F" in here:
                    for t in range(TILES):
                        wait(dve, "yT_hi_ready", f, t + 1)
                        cols = slice(t * P, (t + 1) * P)
                        dve.tensor_tensor(yT_lo[:, :, cols],
                                          bank("yT", t)[:, :].rearrange("p (c q) -> p c q", c=CHUNKS),
                                          yT_hi[:, :, cols].bitcast(F32), ALU.subtract
                                          ).then_inc(S["yT_lo_ready"], 1)
                if here == "ANX":
                    split_lo(dve, 5)
                    split_lo(dve, 6)
                if "A" in here:
                    maxima_of(i, range(0, 4))
                    if "N" in here and "F" in here:
                        rotate_queries(n, 0, 0, "A" in here)
                    maxima_of(i, range(4, 8))
                    if "N" in here and "F" in here:
                        rotate_queries(n, 0, 1, "A" in here)
                    maxima_of(i, range(8, HEADS))
                if here == "ANX":
                    split_lo(dve, 7)
                if "N" in here:
                    if "F" not in here:
                        rotate_queries(n, 0, 0, "A" in here)
                        rotate_queries(n, 0, 1, "A" in here)
                    rotate_queries(n, 1, 0, "A" in here)
                    rotate_queries(n, 1, 1, "A" in here)
                    rotate_keys(n)
                if here == "ANX":
                    for c in (9, 10):
                        split_lo(dve, c)
                if "F" in here:
                    route(f)
                    choose(f)
                if "N" in here and "F" not in here:
                    low_queries(n, 0)
                    low_queries(n, 1)
                    low_keys(n)
                if here == "ANX":
                    split_lo(dve, 11)
                if "A" in here:
                    inverse_sums(i, 0)
                    quotient(i, 0)
                if "N" in here and "F" in here:
                    low_queries(n, 0)
                if "A" in here:
                    quotient_lo(i, 0)
                    inverse_sums(i, 1)
                if "N" in here and "F" in here:
                    low_queries(n, 1)
                if "A" in here:
                    quotient(i, 1)
                if "N" in here and "F" in here:
                    low_keys(n)
                if "F" in here:
                    v_low(f)
                if "A" in here:
                    quotient_lo(i, 1)
                if "F" in here:
                    spread_v(f, i if "A" in here else None)
                if here == "NX":
                    dve.wait_ge(S["gated"], 1)
                    dve.tensor_scalar(gated_bias[:, :], gated_bias[:, :], gates[:, 1:2], None, ALU.mult
                                      ).then_inc(S["gated"], 1)
                if "A" in here:
                    residual(i)
                if "X" in here:
                    statistics(n + 1)
                if "F" in here:
                    result(f)

            run(dve, step)

        @block.gpsimd
        def _(pool):
            def step(i, here, before):
                f, n = i - 1, i + 1

                def root(batch):
                    wait(pool, "rms_ready", batch)
                    flat = rms[:, :, :].rearrange("p a t -> p (a t)")
                    pool.tensor_tensor(flat, flat, minus_half[:, :], ALU.pow).then_inc(S["rooted"], 1)

                if here == "NX":
                    pool.memset(minus_half[:, :], -0.5).then_inc(S["exponents"], 1)
                    pool.wait_ge(S["exponents"], 1)
                if here == "NX":
                    root(0)
                    for c in LO_BY_POOL[:-1]:
                        split_lo(pool, c)
                    root(1)
                    split_lo(pool, LO_BY_POOL[-1])
                if "F" in here:
                    wait(pool, "x1_ready", f)
                    wait(pool, "x_out_free", f)
                    pool.wait_ge(S["gated"], 2)
                    pool.tensor_tensor(x_out[:, :, :], x_res[:, :, :],
                                       gated_bias[:, :].unsqueeze(1).broadcast_to([P, TILES, DIM]), ALU.add
                                       ).then_inc(S["biased"], 1)
                if "A" in here:
                    for u in range(8):
                        t, g = u // KV, u % KV
                        block_ = (probs1[:, g, 1, :] if t else probs0[:, g, :]).rearrange("p (n q) -> p n q", n=GROUP)
                        settled_wait(pool, "exp_done", i, 5 + 2 * g if t else g + 1)
                        pool.affine_select(out=block_, in_=block_, compare_op=ALU.is_ge, fill=0.0, base=0,
                                           pattern=[[0, GROUP], [1, P]], channel_multiplier=-1
                                           ).then_inc(S["masked"], 1)
                if "F" in here:
                    wait(pool, "v_lo_ready", f)
                    if "A" in here:
                        wait(pool, "pv_done", i)
                    for k in range(2):
                        js = slice(4 * k, 4 * k + 4)
                        pool.tensor_tensor(u_lo[:, js, :], spread[:, js, :],
                                           v_lo[:, :].bitcast(F32).unsqueeze(1).broadcast_to([P, 4, SEQ]), ALU.mult
                                           ).then_inc(S["u_lo_ready"], 1)
                if "A" in here:
                    for t in range(TILES):
                        wait(pool, "var_ready", i, t + 1)
                        pool.tensor_tensor(r_rms[:, t:t + 1], r_rms[:, t:t + 1], minus_half[:, 0:1], ALU.pow
                                           ).then_inc(S["y_rooted"], 1)
                if "X" in here and here != "NX":
                    root(n + 1)

            run(pool, step)


W_PIECES = [("o", 0), ("o", 1), ("a", 0), ("a", 1), ("a", 2), ("a", 3), ("w", 0), ("w", 1),
            ("b", 0), ("b", 1), ("b", 2), ("b", 3)]
PIECE = 1024
LO_BY_POOL, LO_BY_DVE, X_OUT_LAST = (0, 1, 2, 3, 4, 8), (5, 6, 7, 9, 10, 11), 8


def w_part(w, c):
    name, k = W_PIECES[c]
    return w[name][:, :, :].rearrange("p a b -> p (a b)")[:, k * PIECE:(k + 1) * PIECE]


def constants():
    t = np.zeros((P, N_CONST), np.float32)

    def put(name, value):
        t[:, slice(*CONST_COLS[name])] = np.asarray(value, np.float32).reshape(P, -1)

    r = np.arange(P)
    put("ident", np.eye(P))
    put("spread_sum", (r[:, None] % RANK == r[None, :] % RANK) / TOPK ** 2)
    col = np.arange(HD)
    put("pick", np.stack([col[None, :] == parity * PER_CHUNK + r[:, None] // RANK for parity in range(2)], 1))
    k = np.arange(P)
    diagonal = np.where(k[None, :] <= r[:, None], 0.0, NEG)
    put("mask", np.concatenate([np.zeros((P, P)), diagonal], 1))
    inv = (np.float32(1.0) / np.float32(10000.0) ** (np.arange(0, HD, 2, dtype=np.float32) / np.float32(HD)))
    freqs = np.outer(np.arange(SEQ, dtype=np.float32), inv.astype(np.float32)).astype(np.float32)
    cos = np.concatenate([np.cos(freqs), np.cos(freqs)], 1)
    sin = np.concatenate([-np.sin(freqs), np.sin(freqs)], 1)
    put("cos", cos.reshape(TILES, P, HD).transpose(1, 0, 2))
    put("sin", sin.reshape(TILES, P, HD).transpose(1, 0, 2))
    j = np.arange(ROUTES)
    row = HD * (j // 2) + (j % 2) * PER_CHUNK
    put("expand", r[:, None, None] == row[None, :, None] + r[None, None, :] // RANK)
    return t


def kernel(**inputs):
    import concourse.bacc as bacc
    from concourse.bass_utils import run_bass_kernel_spmd

    w_out, A, B, W = (np.asarray(inputs[k]) for k in ("L0_xattn_w_out", "L0_ffn_A", "L0_ffn_B", "L0_ffn_W"))
    o = w_out.reshape(DIM, KV, GROUP, HD).transpose(1, 3, 2, 0).reshape(P, CHUNKS * DIM)
    at = A.reshape(ADAPTERS * RANK, CHUNKS, P).transpose(2, 1, 0).reshape(P, -1)
    wt = W.reshape(DIM, CHUNKS, P).transpose(2, 1, 0).reshape(P, -1)
    bt = B.transpose(0, 2, 1).reshape(ROUTES, P, DIM).transpose(1, 0, 2).reshape(P, -1)
    pieces = np.concatenate([o, at, wt, bt], 1).reshape(P, len(W_PIECES), PIECE).transpose(1, 0, 2)
    given = {
        "x": inputs["x"], "ctx": inputs["ctx_512"], "weights": pieces, "const": constants(),
        "qw": np.asarray(inputs["L0_xattn_q_norm_w"]).reshape(1, DIM),
        "kw": np.asarray(inputs["L0_xattn_k_norm_w"]).reshape(1, CTX),
        "bias": np.asarray(inputs["L0_ffn_bias"]).reshape(1, DIM),
        "g_x": np.asarray(inputs["g_xattn"]).reshape(1, 1), "g_f": np.asarray(inputs["g_ffn"]).reshape(1, 1),
    }
    nc = bacc.Bacc("TRN2", target_bir_lowering=False, num_devices=1)
    arrays, a = {}, {}
    for name, value in given.items():
        value = np.ascontiguousarray(value)
        arrays[f"in_{name}"] = value
        a[name] = nc.dram_tensor(f"in_{name}", value.shape, mybir.dt.from_np(value.dtype), kind="ExternalInput").ap()
    a["out"] = nc.dram_tensor("out_0", (BATCHES, SEQ, DIM), F32, kind="ExternalOutput").ap()
    build(nc, a)
    r = run_bass_kernel_spmd(nc, [arrays], core_ids=[0])
    return r.results[0]["out_0"]
```

```python
import numpy as np

import concourse.bass as bass
from concourse import mybir
from contextlib import ExitStack

F32 = mybir.dt.float32
F32R = mybir.dt.float32r
BF16 = mybir.dt.bfloat16
ALU = mybir.AluOpType
ACT = mybir.ActivationFunctionType
AX = mybir.AxisListType

P = 128
BATCHES, SEQ, DIM = 8, 256, 512
TILES = SEQ // P
HEADS, KV = 16, 4
HD = DIM // HEADS
GROUP = HEADS // KV
CTX = KV * HD
CHUNKS = DIM // P
ADAPTERS, RANK, TOPK = 64, 16, 4
PER_CHUNK = P // RANK
ROUTES = ADAPTERS // PER_CHUNK
EPS = 1e-5
SCALE = HD ** -0.5
NEG = -1e30
LOWEST = -3.0e38
SHIFT_ROW = 3 * HD

CONST_COLS = {}
_at = 0
for _name, _n in (("ident", P), ("spread_sum", P), ("pick", 2 * HD), ("mask", 2 * P), ("cos", TILES * HD),
                  ("sin", TILES * HD), ("expand", ROUTES * P)):
    CONST_COLS[_name] = (_at, _at + _n)
    _at += _n
N_CONST = _at
N_KEPT = CONST_COLS["mask"][1]

BANKS = 6


def _unit_order():
    u = []
    for v in range(4):
        u += [("A", "scores", 4 * v + k) for k in range(4)] + [("F", "vecs", v)]
    u += [("A", "maxT", 0), ("F", "ssq", 0), ("F", "normT", 0)]
    u += [("A", "st", n) for n in range(4)]
    u += [("F", "maskT", 0)] + [("A", "st", n) for n in range(4, 6)]
    u += [("F", "spread", v) for v in range(4)] + [("A", "st", n) for n in range(6, 12)]
    u += [("A", "pv", 0), ("A", "pv", 1), ("N", "qkT", 0), ("N", "qkT", 1), ("N", "qkT", 2)]
    u += [("A", "pv", 2), ("A", "pv", 3), ("F", "vsum", 0)]
    u += [("A", "yT", 0), ("A", "yT", 1), ("A", "proj", 0), ("A", "proj", 1)]
    return u


UNITS = _unit_order()
PLACE = {(kind, n): at for at, (_, kind, n) in enumerate(UNITS)}


def bank_of(kind, n):
    return PLACE[(kind, n)] % BANKS


def held_before(kind, n, here, before):
    at = PLACE[(kind, n)]
    for k in range(at - 1, -1, -1):
        if k % BANKS == at % BANKS and UNITS[k][0] in here:
            return (*UNITS[k], 0)
    for k in range(len(UNITS) - 1, -1, -1):
        if k % BANKS == at % BANKS and UNITS[k][0] in before:
            return (*UNITS[k], 1)
    return None


def build(nc, a):
    ctx = ExitStack()
    with ctx:
        def sb(name, shape, dt=F32):
            return ctx.enter_context(nc.sbuf_tensor(name, [P, *shape], dt))

        def sem(name):
            return ctx.enter_context(nc.semaphore(name))

        arena = (nc.sbuf_base + 31) // 32 * 32
        probs0 = sb("probs0", [KV, GROUP * P])
        probs1 = sb("probs1", [KV, 2, GROUP * P])
        half = KV * GROUP * P * 4
        o_hi = nc.alloc_sbuf_tensor_at("o_hi", [P, TILES, DIM], F32R, offset=arena)
        o_lo = nc.alloc_sbuf_tensor_at("o_lo", [P, TILES, DIM], F32R, offset=arena + half // 2)
        u_hi = nc.alloc_sbuf_tensor_at("u_hi", [P, ROUTES, SEQ], F32R, offset=arena + half)
        u_lo = nc.alloc_sbuf_tensor_at("u_lo", [P, ROUTES, SEQ], F32R, offset=arena + 2 * half)
        squares = probs1[:, :, :, :].rearrange("p g k c -> p (g k c)")[:, 0:ROUTES * SEQ].rearrange(
            "p (j t) -> p j t", j=ROUTES)
        expand_f = probs1[:, :, :, :].rearrange("p g k c -> p (g k c)")[:, 0:ROUTES * P]

        w_shape = {"o": (CHUNKS, DIM), "a": (CHUNKS, ADAPTERS * RANK), "w": (CHUNKS, DIM), "b": (ROUTES, DIM)}
        w_hi = {k: sb(f"w_{k}_hi", s, F32R) for k, s in w_shape.items()}
        w_lo = {k: sb(f"w_{k}_lo", s, F32R) for k, s in w_shape.items()}

        x_next = sb("x_next", [TILES, DIM])
        x_res = sb("x_res", [TILES, DIM])
        x_out = sb("x_out", [TILES, DIM])
        ctx_next = sb("ctx_next", [TILES, CTX])
        values = sb("values", [TILES, CTX])

        q_cos = sb("q_cos", [TILES, DIM])
        q_sin = sb("q_sin", [TILES, DIM])
        k_cos = sb("k_cos", [TILES, CTX])
        k_sin = sb("k_sin", [TILES, CTX])
        const = sb("const", [N_KEPT])
        ident, spread_sum, pick, mask = (const[:, slice(*CONST_COLS[k])]
                                         for k in ("ident", "spread_sum", "pick", "mask"))
        ident_bf = sb("ident_bf", [P], BF16)
        expand = sb("expand", [ROUTES, P], BF16)
        ones = sb("ones", [HD])
        gated_bias = sb("gated_bias", [DIM])
        gates = sb("gates", [2])
        minus_half = sb("minus_half", [2 * TILES])

        scratch = sb("scratch", [TILES, DIM])
        roped = sb("roped", [TILES, DIM])
        k_norm = sb("k_norm", [TILES, CTX])
        k_rope = sb("k_rope", [TILES, CTX])
        stats = sb("stats", [TILES, 6])
        aggr = sb("aggr", [TILES, 2])
        k_stats = sb("k_stats", [TILES, 6])
        k_aggr = sb("k_aggr", [TILES, 2])
        rms = sb("rms", [2, TILES])
        r_stats = sb("r_stats", [TILES, 6])
        r_aggr = sb("r_aggr", [TILES, 2])
        r_rms = sb("r_rms", [TILES])
        inverse = sb("inverse", [DIM // HD])
        q_stack = sb("q_stack", [HEADS, SEQ], F32R)
        k_stack = sb("k_stack", [KV, SEQ], F32R)
        maxima = sb("maxima", [TILES * HEADS])
        minus_max = sb("minus_max", [P])

        y_arena = (nc.sbuf_base + 31) // 32 * 32
        yT_hi = sb("yT_hi", [CHUNKS, SEQ], F32R)
        yT_lo = sb("yT_lo", [CHUNKS, SEQ], F32R)
        vecs = sb("vecs", [ROUTES, SEQ])
        q_hi, q_lo = vecs[:, 0:CHUNKS, :], vecs[:, CHUNKS:ROUTES, :]
        k_hi, k_lo = roped[:, 0, 0:SEQ], roped[:, 0, SEQ:2 * SEQ]
        spread = sb("spread", [ROUTES, SEQ], BF16)
        ssqT = sb("ssqT", [SEQ])
        norms = sb("norms", [TILES, ADAPTERS + 8])
        top = sb("top", [TILES, 8])
        wanted = sb("wanted", [TILES, 8])
        replaced = sb("replaced", [TILES, ADAPTERS + 8])
        chosen = sb("chosen", [TILES, P], BF16)
        chosenT = sb("chosenT", [SEQ], BF16)
        v_hi = sb("v_hi", [SEQ], F32R)
        v_lo = sb("v_lo", [SEQ], F32R)

        qw_b = vecs[:, 4:6, :].rearrange("p a b -> p (a b)")
        kw_b = vecs[:, 6, 0:CTX]
        trig = ssqT[:, 0:2 * TILES * HD]
        stage = [x_out[:, :, :].rearrange("p a b -> p (a b)"),
                 spread[:, :, :].rearrange("p a b -> p (a b)").bitcast(F32),
                 *(nc.alloc_sbuf_tensor_at(f"in_yT_{k}", [P, PIECE], F32, offset=y_arena + 4 * PIECE * k)[:, :]
                   for k in range(2)),
                 *(probs1[:, g, :, :].rearrange("p k c -> p (k c)") for g in range(1, KV)),
                 x_res[:, :, :].rearrange("p a b -> p (a b)")]

        banks = [ctx.enter_context(nc.psum_tensor(f"bank{k}", [P, 512], F32)) for k in range(BANKS)]
        acc = [ctx.enter_context(nc.psum_tensor(f"acc{t}", [P, 512], F32)) for t in range(TILES)]

        def bank(kind, n):
            return banks[bank_of(kind, n)]

        PER = dict(
            x_loaded=16, ctx_loaded=16, values_loaded=16, res_loaded=16,
            stacked0=96, stacked1=96, stacked2=96, stacked3=96, shift_stacked=32, x_out_free=32,
            yT_done=2, scores_done=16, vecs_done=4, ssq_done=1, maxT_done=1, normT_done=1, st_done=12,
            maskT_done=1, spread_done=4, pv_done=4, vsum_done=1, qkT_done=3, proj_done=2, acc_done=2,
            yT_hi_ready=2, vecs_ready=4, squared=4, ssqT_ready=1, minus_ready=1, exp_done=12,
            chosenT_ready=1, spread_ready=4, o_hi_ready=2, v_hi_ready=1, q_hi_ready=2, k_hi_ready=1,
            stat_step=10, rms_ready=1, q_step=8, q_roped=2, k_step=5, k_roped=1, q_lo_ready=2, k_lo_ready=1,
            maxed=32, sums_taken=2, norm_step=4, quotient_ready=2, o_lo_ready=2,
            x1_ready=2, y_step=4, var_ready=2, y_ready=2, yT_lo_ready=2,
            norms_taken=1, route_step=5, routed=1, picked=4, vsum_ready=1, v_lo_ready=1, u_hi_ready=2,
            out_ready=2,
            rooted=1, masked=8, y_rooted=2, u_lo_ready=2, biased=1)
        ONCE = ("const_loaded", "trig_loaded", "expand_loaded", "vectors_loaded", "gates_loaded",
                *(f"w{s}_loaded" for s in range(len(stage))), "w_hi_done", "w_lo_by_pool", "w_lo_by_dve",
                *(f"first_keys{g}" for g in range(KV)),
                "q_tables", "k_tables", "gated", "constants", "expand_ready", "fills", "exponents")
        S = {k: sem(k) for k in (*PER, *ONCE)}

        def wait(eng, name, batch, done=None):
            eng.wait_ge(S[name], PER[name] * batch + (PER[name] if done is None else done))

        def settled_wait(eng, name, batch, done=None):
            value = PER[name] * batch + (PER[name] if done is None else done)
            if not isinstance(batch, int):
                value = eng.compute_val(value)
                eng.wait_ge(S[name], 1)
            eng.wait_ge(S[name], value)

        def stack_queries(eng, g):
            for part, qs in enumerate((q_hi, q_lo, q_hi)):
                eng.dma_start(q_stack[part * HD:(part + 1) * HD, g * GROUP:(g + 1) * GROUP, :].bitcast(F32),
                              qs[g * HD:(g + 1) * HD]).then_inc(S[f"stacked{g}"], 16)

        def stack_keys(eng, g, name):
            for part, ks in enumerate((k_hi, k_hi, k_lo)):
                eng.dma_start(k_stack[part * HD:(part + 1) * HD, g, :].bitcast(F32),
                              ks[g * HD:(g + 1) * HD]).then_inc(S[name], 16)

        def load_weights(eng, c):
            s = c % len(stage)
            if c >= len(stage):
                wait_split(eng, c - len(stage))
            eng.dma_start(stage[s], a["weights"][c]).then_inc(S[f"w{s}_loaded"], 16)

        def split_lo(eng, c):
            s = c % len(stage)
            eng.wait_ge(S["w_hi_done"], c + 1)
            ins = eng.tensor_tensor(w_part(w_lo, c), stage[s], w_part(w_hi, c).bitcast(F32), ALU.subtract)
            if c == X_OUT_LAST:
                ins.then_inc(S["x_out_free"], 32)
            else:
                ins.then_inc(S["w_lo_by_pool" if c in LO_BY_POOL else "w_lo_by_dve"], 1)

        def wait_split(eng, c):
            if c == X_OUT_LAST:
                eng.wait_ge(S["x_out_free"], 32)
            elif c in LO_BY_POOL:
                eng.wait_ge(S["w_lo_by_pool"], LO_BY_POOL.index(c) + 1)
            else:
                eng.wait_ge(S["w_lo_by_dve"], LO_BY_DVE.index(c) + 1)

        def wait_all_split(eng):
            eng.wait_ge(S["x_out_free"], 32)
            eng.wait_ge(S["w_lo_by_pool"], len(LO_BY_POOL))
            eng.wait_ge(S["w_lo_by_dve"], len(LO_BY_DVE))

        READ = {"yT": lambda n: ("yT_lo_ready", n + 1), "scores": lambda n: ("maxed", 2 * n + 2),
                "vecs": lambda n: ("vecs_ready", n + 1), "ssq": lambda n: ("ssqT_ready", 1),
                "maxT": lambda n: ("minus_ready", 1), "normT": lambda n: ("norms_taken", 1),
                "st": lambda n: ("exp_done", n + 1), "maskT": lambda n: ("chosenT_ready", 1),
                "spread": lambda n: ("spread_ready", n + 1),
                "pv": lambda n: (("sums_taken", "quotient_ready")[n % 2], n // 2 + 1),
                "vsum": lambda n: ("v_lo_ready", 1),
                "qkT": lambda n: ("k_lo_ready", 1) if n == 2 else ("q_lo_ready", n + 1),
                "proj": lambda n: ("x1_ready", n + 1)}
        AHEAD = {"A": 0, "F": -1, "N": 1}

        def heads_of(u):
            g, t, pair = u // 4, u // 2 % 2, u % 2
            return (GROUP * g + 2 * pair, GROUP * g + 2 * pair + 1), t

        def tile_of(u):
            return (u, 0, 0) if u < KV else ((u - KV) // 2, 1 - (u - KV) % 2, 1)

        def chain(eng, name, batch):
            count = [0]

            def did(ins):
                count[0] += 1
                assert count[0] <= PER[name]
                ins.then_inc(S[name], 1)

            def settle():
                wait(eng, name, batch, count[0])
            return did, settle

        def halves(ap, s):
            return ap.rearrange("p (g n s d) -> p g n s d", g=KV, s=2, d=HD // 2)[:, :, :, s, :]

        def run(eng, step):
            step(-1, "NX", "")
            step(0, "ANX", "N")
            with eng.Fori(1, BATCHES - 2) as i:
                step(i, "FANX", "AN")
            step(BATCHES - 2, "FAN", "FAN")
            step(BATCHES - 1, "FA", "FAN")
            step(BATCHES, "F", "FA")

        def tables(eng, name, heads, w, to_cos, to_sin):
            cos, sin = (trig[:, k * TILES * HD:(k + 1) * TILES * HD] for k in range(2))
            hd = HD // 2
            halves_of = lambda ap, s: ap.rearrange("p (h s d) -> p h s d", h=heads, s=2)[:, :, s, :]
            eng.wait_ge(S["trig_loaded"], 16)
            eng.wait_ge(S["vectors_loaded"], 32)
            for t in range(TILES):
                for s in range(2):
                    wide = lambda ap: ap[:, t * HD + s * hd:t * HD + (s + 1) * hd].unsqueeze(1).broadcast_to(
                        [P, heads, hd])
                    for to, of, table in ((to_cos, s, cos), (to_sin, 1 - s, sin)):
                        eng.tensor_tensor(halves_of(to[:, t, :], s), halves_of(w, of), wide(table), ALU.mult
                                          ).then_inc(S[name], 1)

        block = ctx.enter_context(nc.Block())

        @block.sync
        def _(sp):
            def load_x(n):
                sp.dma_start(x_next[:, :, :], a["x"][n].rearrange("(t p) c -> p t c", p=P)
                             ).then_inc(S["x_loaded"], 16)
                sp.dma_start(ctx_next[:, :, :], a["ctx"][n].rearrange("(t p) c -> p t c", p=P)
                             ).then_inc(S["ctx_loaded"], 16)

            def load_values(b):
                sp.dma_start(values[:, :, :], a["ctx"][b].rearrange("(t p) c -> p t c", p=P)
                             ).then_inc(S["values_loaded"], 16)

            def load_res(b):
                sp.dma_start(x_res[:, :, :], a["x"][b].rearrange("(t p) c -> p t c", p=P)
                             ).then_inc(S["res_loaded"], 16)

            def step(i, here, before):
                if here == "NX":
                    load_x(0)
                    sp.dma_start(trig, a["const"][:, CONST_COLS["cos"][0]:CONST_COLS["sin"][1]]
                                 ).then_inc(S["trig_loaded"], 16)
                    sp.dma_start(qw_b, a["qw"].broadcast_to([P, DIM])).then_inc(S["vectors_loaded"], 16)
                    sp.dma_start(kw_b, a["kw"].broadcast_to([P, CTX])).then_inc(S["vectors_loaded"], 16)
                    sp.dma_start(const[:, :], a["const"][:, 0:N_KEPT]).then_inc(S["const_loaded"], 16)
                    sp.dma_start(gates[:, 0:1], a["g_x"].broadcast_to([P, 1])).then_inc(S["gates_loaded"], 16)
                    sp.dma_start(gates[:, 1:2], a["g_f"].broadcast_to([P, 1])).then_inc(S["gates_loaded"], 16)
                    sp.dma_start(gated_bias[:, :], a["bias"].broadcast_to([P, DIM])).then_inc(S["gates_loaded"], 16)
                    sp.dma_start(expand_f, a["const"][:, slice(*CONST_COLS["expand"])]
                                 ).then_inc(S["expand_loaded"], 16)
                if "A" in here:
                    if "A" in before:
                        wait(sp, "pv_done", i - 1)
                    load_values(i)
                    if "F" in here:
                        wait(sp, "biased", i - 1)
                        wait(sp, "y_ready", i - 1)
                    if here != "ANX":
                        load_res(i)
                    wait(sp, "minus_ready", i)
                    for t in range(TILES):
                        sp.dma_start(q_stack[SHIFT_ROW:SHIFT_ROW + 1, :, t * P:(t + 1) * P].bitcast(F32),
                                     minus_max[t * HEADS:(t + 1) * HEADS, :]).then_inc(S["shift_stacked"], 16)
                    if here == "ANX":
                        for c in range(len(stage), len(W_PIECES)):
                            load_weights(sp, c)
                        wait(sp, "k_roped", 1)
                        load_x(2)
                        wait_split(sp, 7)
                        load_res(i)
                if "X" in here and "F" in here:
                    wait(sp, "k_roped", i + 1)
                    load_x(i + 2)
                if "N" in here:
                    wait(sp, "k_lo_ready", i + 1)
                    wait(sp, "q_lo_ready", i + 1)
                    for g in range(KV):
                        stack_queries(sp, g)
                        if here != "NX":
                            stack_keys(sp, g, f"stacked{g}")
                if here == "NX":
                    load_x(1)
                if "F" in here:
                    for t in range(TILES):
                        wait(sp, "out_ready", i - 1, t + 1)
                        sp.dma_start(a["out"][i - 1][t * P:(t + 1) * P, :], x_out[:, t, :]
                                     ).then_inc(S["x_out_free"], 16)

            run(sp, step)
            wait(sp, "x_out_free", BATCHES)

        @block.tensor
        def _(pe):
            def step(i, here, before):
                def take(kind, n):
                    held = held_before(kind, n, here, before)
                    if held:
                        stage_, k, m, ago = held
                        name, count = READ[k](m)
                        wait(pe, name, i + AHEAD[stage_] - ago, count)
                    return bank(kind, n)

                def products(out, terms, name, first=True, last=True):
                    for k, (l, r) in enumerate(terms):
                        ins = nc.tensor.matmul(out, l, r, start=(first and k == 0),
                                               stop=(last and k == len(terms) - 1), skip_group_check=True)
                    if name:
                        ins.then_inc(S[name], 1)

                f, n = i - 1, i + 1

                def y_transposed(t):
                    wait(pe, "y_ready", i, t + 1)
                    ps = take("yT", t)
                    for c in range(CHUNKS):
                        ins = nc.tensor.transpose(ps[:, c * P:(c + 1) * P], scratch[:, t, c * P:(c + 1) * P], ident)
                    ins.then_inc(S["yT_done"], 1)

                def scores(u):
                    heads, t = heads_of(u)
                    if u % GROUP == 0:
                        g = heads[0] // GROUP
                        if here == "ANX":
                            pe.wait_ge(S[f"first_keys{g}"], 48)
                            pe.sem_inc(S[f"stacked{g}"], 48)
                        wait(pe, f"stacked{g}", i)
                    ps = take("scores", u)
                    for k, h in enumerate(heads):
                        ins = nc.tensor.matmul(ps[:, k * SEQ:(k + 1) * SEQ],
                                               q_stack[0:SHIFT_ROW, h, t * P:(t + 1) * P],
                                               k_stack[0:SHIFT_ROW, h // GROUP, :], start=True, stop=True)
                    ins.then_inc(S["scores_done"], 1)

                def adapter_vecs(v):
                    if v == 0:
                        wait(pe, "yT_hi_ready", f)
                    ps = take("vecs", v)
                    for k in range(2):
                        cols = slice((2 * v + k) * P, (2 * v + k + 1) * P)
                        terms = [(w[:, c, cols], y[:, c, :]) for w, y in
                                 ((w_hi["a"], yT_hi), (w_lo["a"], yT_hi), (w_hi["a"], yT_lo)) for c in range(CHUNKS)]
                        out = ps[:, k * SEQ:(k + 1) * SEQ]
                        products(out, terms[:2 * CHUNKS], None, last=False)
                        if v == 0 and k == 0:
                            wait(pe, "yT_lo_ready", f)
                        products(out, terms[2 * CHUNKS:], "vecs_done" if k else None, first=False)

                def squared_norms():
                    wait(pe, "squared", f)
                    ps = take("ssq", 0)
                    for parity in range(2):
                        for q in range(4):
                            ins = nc.tensor.matmul(ps[q * HD:(q + 1) * HD, 0:SEQ],
                                                   pick[:, parity * HD:(parity + 1) * HD],
                                                   squares[:, 2 * q + parity, :], start=(parity == 0),
                                                   stop=(parity == 1), skip_group_check=True)
                    ins.then_inc(S["ssq_done"], 1)

                def norms_transposed():
                    wait(pe, "ssqT_ready", f)
                    ps = take("normT", 0)
                    for t in range(TILES):
                        ins = nc.tensor.transpose(ps[:, t * P:(t + 1) * P], ssqT[:, t * P:(t + 1) * P], ident)
                    ins.then_inc(S["normT_done"], 1)

                def maxima_transposed():
                    wait(pe, "maxed", i)
                    ps = take("maxT", 0)
                    nc.tensor.transpose(ps[0:TILES * HEADS, 0:P], maxima[:, :], ident).then_inc(S["maxT_done"], 1)

                def base(t, start, end):
                    if start == end:
                        return
                    if t == 1 and start == 0 and not A:
                        wait(pe, "out_ready", f - 1)
                    toks = slice(t * P, (t + 1) * P)
                    terms = [(y[:, c, toks], w[:, c, :]) for y, w in
                             ((yT_hi, w_hi["w"]), (yT_lo, w_hi["w"]), (yT_hi, w_lo["w"])) for c in range(CHUNKS)]
                    products(acc[t][:, :], terms[start:end], None, first=(start == 0), last=False)

                def scores_T(u):
                    if u == 0:
                        wait(pe, "shift_stacked", i)
                    ps = take("st", u)
                    g, kb, t = tile_of(u)
                    nc.tensor.matmul(ps[:, :], k_stack[0:SHIFT_ROW + 1, g, kb * P:(kb + 1) * P],
                                     q_stack[0:SHIFT_ROW + 1, g * GROUP:(g + 1) * GROUP, t * P:(t + 1) * P],
                                     start=True, stop=True).then_inc(S["st_done"], 1)

                def mask_transposed():
                    wait(pe, "routed", f)
                    ps = take("maskT", 0)[:, :].bitcast(BF16)
                    for t in range(TILES):
                        ins = nc.tensor.transpose(ps[:, t * P:(t + 1) * P], chosen[:, t, :], ident_bf[:, :])
                    ins.then_inc(S["maskT_done"], 1)

                def mask_spread(v):
                    if v == 0:
                        wait(pe, "chosenT_ready", f)
                    ps = take("spread", v)
                    for k in range(2):
                        ins = nc.tensor.matmul(ps[:, k * SEQ:(k + 1) * SEQ], expand[:, 2 * v + k, :], chosenT[:, :],
                                               start=True, stop=True)
                    ins.then_inc(S["spread_done"], 1)

                def attend(u):
                    t, with_values = u // 2, u % 2
                    if u == 0:
                        wait(pe, "values_loaded", i)
                    if not with_values:
                        wait(pe, "masked", i, 4 * (t + 1))
                        wait(pe, "exp_done", i, (4, 12)[t])
                    ps = take("pv", u)
                    for kb in range(t + 1):
                        for g in range(KV):
                            pr = probs1[:, g, kb, :] if t else probs0[:, g, :]
                            l = values[:, kb, g * HD:(g + 1) * HD] if with_values else ones[:, :]
                            ins = nc.tensor.matmul(ps[g * HD:(g + 1) * HD, :], l, pr, start=(kb == 0),
                                                   stop=(kb == t), skip_group_check=True)
                    ins.then_inc(S["pv_done"], 1)

                def chosen_sum():
                    if not A:
                        ps = take("vsum", 0)
                        for j in range(ROUTES):
                            if j % 2 == 0:
                                wait(pe, "picked", f, j // 2 + 1)
                            ins = nc.tensor.matmul(ps[:, 0:SEQ], spread_sum, vecs[:, j, :], start=(j == 0),
                                                   stop=(j == ROUTES - 1))
                        ins.then_inc(S["vsum_done"], 1)
                        return
                    wait(pe, "vsum_ready", f)
                    ps = take("vsum", 0)
                    nc.tensor.matmul(ps[:, 0:SEQ], spread_sum, ssqT[:, :], start=True, stop=True
                                     ).then_inc(S["vsum_done"], 1)

                def qk_transposed(u):
                    if u < TILES:
                        wait(pe, "q_roped", n, u + 1)
                    else:
                        wait(pe, "k_roped", n)
                    ps = take("qkT", u)
                    for c in range(CHUNKS if u < TILES else TILES):
                        src = roped[:, u, c * P:(c + 1) * P] if u < TILES else k_rope[:, c, :]
                        ins = nc.tensor.transpose(ps[:, c * P:(c + 1) * P], src, ident)
                    ins.then_inc(S["qkT_done"], 1)

                def project(t):
                    wait(pe, "o_hi_ready", i, t + 1)
                    ps = take("proj", t)
                    terms = [(o[:, t, c * P:(c + 1) * P], w[:, c, :]) for o, w in
                             ((o_hi, w_hi["o"]), (o_hi, w_lo["o"]), (o_lo, w_hi["o"])) for c in range(CHUNKS)]
                    products(ps[:, :], terms[:2 * CHUNKS], None, last=False)
                    wait(pe, "o_lo_ready", i, t + 1)
                    products(ps[:, :], terms[2 * CHUNKS:], "proj_done", first=False)

                def delta(t, between=None):
                    toks = slice(t * P, (t + 1) * P)
                    for k in range(2):
                        if t == 0:
                            wait(pe, "u_hi_ready", f, k + 1)
                        products(acc[t][:, :], [(u_hi[:, j, toks], w[:, j, :]) for w in (w_hi["b"], w_lo["b"])
                                                for j in range(4 * k, 4 * k + 4)], None, first=False, last=False)
                        if k == 0 and between:
                            between()
                    if t == 0:
                        wait(pe, "u_lo_ready", f)
                    products(acc[t][:, :], [(u_lo[:, j, toks], w_hi["b"][:, j, :]) for j in range(ROUTES)],
                             "acc_done", first=False)

                def both_y_transposed():
                    y_transposed(0)
                    y_transposed(1)

                if here == "NX":
                    pe.wait_ge(S["const_loaded"], 16)
                    pe.wait_ge(S["constants"], 1)
                    pe.wait_ge(S["fills"], 5)
                F, A, N = "F" in here, "A" in here, "N" in here
                for v in range(4):
                    if A:
                        for k in range(4):
                            scores(4 * v + k)
                    if F:
                        adapter_vecs(v)
                if F:
                    base(0, 0, 4)
                if A:
                    maxima_transposed()
                if F:
                    squared_norms()
                    base(0, 4, 12 if A else 6)
                    norms_transposed()
                    base(0, 12 if A else 6, 12)
                    base(1, 0, 3)
                if A:
                    for u in range(4):
                        scores_T(u)
                if F:
                    base(1, 3, 5 if A else 3)
                    mask_transposed()
                if A:
                    for u in range(4, 6):
                        scores_T(u)
                if F:
                    base(1, 5 if A else 3, 9 if A else 5)
                    for v in range(4):
                        mask_spread(v)
                    if A:
                        base(1, 9, 12)
                if A and not F:
                    for u in range(6, 10):
                        scores_T(u)
                    attend(0)
                    for u in range(10, 12):
                        scores_T(u)
                    attend(1)
                    for u in range(3):
                        qk_transposed(u)
                elif N and not F:
                    for u in range(3):
                        qk_transposed(u)
                elif A:
                    for u in range(6, 12):
                        scores_T(u)
                    attend(0)
                    attend(1)
                if N and F:
                    for u in range(3):
                        qk_transposed(u)
                if A:
                    attend(2)
                    attend(3)
                if F:
                    chosen_sum()
                    if not A:
                        base(1, 5, 12)
                if A:
                    if here == "ANX":
                        wait_split(pe, 1)
                    project(0)
                    project(1)
                if here == "ANX":
                    wait_all_split(pe)
                    pe.wait_ge(S["expand_ready"], 1)
                if F:
                    delta(0)
                    delta(1, both_y_transposed if A else None)
                elif A:
                    both_y_transposed()

            run(pe, step)

        @block.scalar
        def _(act):
            def split_hi(c):
                act.wait_ge(S[f"w{c % len(stage)}_loaded"], 16 * (c // len(stage) + 1))
                nc.scalar.copy(w_part(w_hi, c), stage[c % len(stage)]).then_inc(S["w_hi_done"], 1)

            def step(i, here, before):
                f, n = i - 1, i + 1

                def exponentials(u):
                    g, kb, t = tile_of(u)
                    to = probs1[:, g, kb, :] if t else probs0[:, g, :]
                    wait(act, "st_done", i, u + 1)
                    nc.scalar.activation(to, bank("st", u)[:, :], ACT.Exp).then_inc(S["exp_done"], 1)

                def quotient_hi(t):
                    wait(act, "quotient_ready", i, t + 1)
                    nc.scalar.copy(o_hi[:, t, :], scratch[:, 1, :]).then_inc(S["o_hi_ready"], 1)

                if here == "NX":
                    act.wait_ge(S["const_loaded"], 16)
                    for c in range(len(stage)):
                        load_weights(act, c)
                    for c in range(3):
                        split_hi(c)
                if here == "ANX":
                    act.wait_ge(S["expand_loaded"], 16)
                    nc.scalar.copy(expand[:, :, :].rearrange("p j c -> p (j c)"), expand_f
                                   ).then_inc(S["expand_ready"], 1)
                    act.wait_ge(S["gates_loaded"], 48)
                    nc.scalar.activation(gates[:, :], gates[:, :], ACT.Tanh).then_inc(S["gated"], 1)
                    for c in range(3, len(stage)):
                        split_hi(c)
                if "F" in here:
                    for v in range(4):
                        ps = bank("vecs", v)[:, :].rearrange("p (k t) -> p k t", k=2)
                        wait(act, "vecs_done", f, v + 1)
                        nc.scalar.activation(squares[:, 2 * v:2 * v + 2, :], ps, ACT.Square).then_inc(S["squared"], 1)
                        if v == 0 and "A" in here:
                            for g in range(KV):
                                wait(act, f"stacked{g}", i)
                        nc.scalar.copy(vecs[:, 2 * v:2 * v + 2, :], ps).then_inc(S["vecs_ready"], 1)
                if "A" in here:
                    wait(act, "maxT_done", i)
                    nc.scalar.mul(minus_max[0:TILES * HEADS, :].bitcast(F32R), bank("maxT", 0)[0:TILES * HEADS, 0:P],
                                  -1.0).then_inc(S["minus_ready"], 1)
                if "F" in here:
                    wait(act, "ssq_done", f)
                    nc.scalar.copy(ssqT[:, :], bank("ssq", 0)[:, 0:SEQ]).then_inc(S["ssqT_ready"], 1)
                if "A" in here:
                    for u in range(4):
                        exponentials(u)
                if "F" in here:
                    wait(act, "maskT_done", f)
                    nc.scalar.copy(chosenT[:, :], bank("maskT", 0)[:, :].bitcast(BF16)[:, 0:SEQ]
                                   ).then_inc(S["chosenT_ready"], 1)
                if here == "ANX":
                    for c in (4, 5, 6):
                        wait_split(act, c)
                if "A" in here:
                    for u in range(4, 6):
                        exponentials(u)
                if "F" in here:
                    for v in range(4):
                        wait(act, "spread_done", f, v + 1)
                        nc.scalar.copy(spread[:, 2 * v:2 * v + 2, :],
                                       bank("spread", v)[:, :].rearrange("p (k t) -> p k t", k=2)
                                       ).then_inc(S["spread_ready"], 1)
                if "A" in here:
                    for u in range(6, 12):
                        exponentials(u)
                if here == "ANX":
                    split_hi(8)

                def high_keys():
                    wait(act, "qkT_done", n)
                    nc.scalar.copy(k_hi.bitcast(F32R), bank("qkT", 2)[:, 0:SEQ]).then_inc(S["k_hi_ready"], 1)

                if "N" in here:
                    if "F" in here:
                        high_keys()
                    for t in range(TILES):
                        wait(act, "qkT_done", n, t + 1)
                        if t == 0 and "F" in here:
                            wait(act, "vsum_ready", f)
                        nc.scalar.copy(q_hi[:, :, t * P:(t + 1) * P].bitcast(F32R),
                                       bank("qkT", t)[:, :].rearrange("p (c q) -> p c q", c=CHUNKS)
                                       ).then_inc(S["q_hi_ready"], 1)
                    if "F" not in here:
                        high_keys()
                if here == "ANX":
                    split_hi(9)
                if "A" in here:
                    quotient_hi(0)
                if "F" in here:
                    wait(act, "vsum_done", f)
                    nc.scalar.copy(v_hi[:, :], bank("vsum", 0)[:, 0:SEQ]).then_inc(S["v_hi_ready"], 1)
                if here == "ANX":
                    split_hi(10)
                    split_hi(11)
                if "A" in here:
                    quotient_hi(1)
                    for t in range(TILES):
                        wait(act, "yT_done", i, t + 1)
                        nc.scalar.copy(yT_hi[:, :, t * P:(t + 1) * P],
                                       bank("yT", t)[:, :].rearrange("p (c q) -> p c q", c=CHUNKS)
                                       ).then_inc(S["yT_hi_ready"], 1)

            run(act, step)

        @block.vector
        def _(dve):
            def statistics(n):
                did, settle = chain(dve, "stat_step", n)
                wait(dve, "x_loaded", n)
                for t in range(TILES):
                    did(dve.bn_stats(stats[:, t, :], x_next[:, t, :]))
                wait(dve, "ctx_loaded", n)
                for t in range(TILES):
                    did(dve.bn_stats(k_stats[:, t, :], ctx_next[:, t, :]))
                settled_wait(dve, "stat_step", n, 4)
                for t in range(TILES):
                    did(dve.bn_aggr(aggr[:, t, :], stats[:, t, :]))
                    did(dve.bn_aggr(k_aggr[:, t, :], k_stats[:, t, :]))
                settle()
                did(dve.tensor_scalar(rms[:, 0, :], aggr[:, :, 1], HD * (1.0 + EPS), HD * EPS * EPS,
                                      ALU.mult, ALU.add))
                did(dve.tensor_tensor(rms[:, 1, :], k_aggr[:, :, 0], k_aggr[:, :, 0], ALU.mult))
                settle()
                dve.scalar_tensor_tensor(out=rms[:, 1, :], in0=k_aggr[:, :, 1], scalar=EPS, in1=rms[:, 1, :],
                                         op0=ALU.add, op1=ALU.add).then_inc(S["rms_ready"], 1)

            normed, product = scratch[:, 0, :], scratch[:, 1, :]

            def rotate_queries(n, t, part, after):
                out = roped[:, t, :].rearrange("p (n g d) -> p g n d", n=GROUP, g=KV)
                heads = lambda ap: ap.rearrange("p (g n d) -> p g n d", g=KV, n=GROUP)
                if part == 0:
                    if t == 0:
                        wait(dve, "rooted", n)
                    dve.tensor_scalar(normed, x_next[:, t, :], aggr[:, t, 0:1], rms[:, 0, t:t + 1],
                                      ALU.subtract, ALU.mult).then_inc(S["q_step"], 1)
                    wait(dve, "q_step", n, 4 * t + 1)
                    for s in range(2):
                        dve.tensor_tensor(halves(product, s), halves(normed, 1 - s), halves(q_sin[:, t, :], s),
                                          ALU.mult).then_inc(S["q_step"], 1)
                else:
                    if t == 0 and after:
                        for g in range(KV):
                            wait(dve, f"stacked{g}", n - 1)
                    dve.tensor_tensor(out, heads(normed), heads(q_cos[:, t, :]), ALU.mult).then_inc(S["q_step"], 1)
                    wait(dve, "q_step", n, 4 * t + 4)
                    dve.tensor_tensor(out, out, heads(product), ALU.add).then_inc(S["q_roped"], 1)

            def rotate_keys(n):
                did, settle = chain(dve, "k_step", n)
                for t in range(TILES):
                    did(dve.tensor_scalar(k_norm[:, t, :], ctx_next[:, t, :], rms[:, 1, t:t + 1], None, ALU.mult))
                settle()
                flat = lambda ap: ap[:, :, :].rearrange("p t c -> p (t c)")
                swap = lambda ap, s: ap.rearrange("p (h s d) -> p h s d", s=2, d=HD // 2)[:, :, s, :]
                did(dve.tensor_tensor(flat(k_rope), flat(k_norm), flat(k_cos), ALU.mult))
                wait(dve, "q_roped", n)
                for s in range(2):
                    did(dve.tensor_tensor(swap(product[:, 0:TILES * CTX], s), swap(flat(k_norm), 1 - s),
                                          swap(flat(k_sin), s), ALU.mult))
                settle()
                dve.tensor_tensor(flat(k_rope), flat(k_rope), product[:, 0:TILES * CTX], ALU.add
                                  ).then_inc(S["k_roped"], 1)

            def maxima_of(b, units):
                for u in units:
                    (heads, t), ps = heads_of(u), bank("scores", u)
                    settled_wait(dve, "scores_done", b, u + 1)
                    if u >= 4:
                        settled_wait(dve, "maxed", b, 2 * u - 6)
                    for k, h in enumerate(heads):
                        keys = (t + 1) * P
                        slot = probs0[:, u % 4, k * SEQ:k * SEQ + keys]
                        dve.tensor_tensor_reduce(slot, ps[:, k * SEQ:k * SEQ + keys],
                                                 mask[:, 2 * P - keys:2 * P], 1.0, LOWEST, ALU.add, ALU.max,
                                                 maxima[:, t * HEADS + h:t * HEADS + h + 1]).then_inc(S["maxed"], 1)

            def route(f):
                did, settle = chain(dve, "route_step", f)
                wait(dve, "normT_done", f)
                dve.tensor_copy(norms[:, :, 0:ADAPTERS].rearrange("p t (q a) -> p t q a", q=4),
                                bank("normT", 0)[:, 0:TILES * P].rearrange("p (t q a) -> p t q a", t=TILES, q=4
                                                                          )[:, :, :, 0:RANK]
                                ).then_inc(S["norms_taken"], 1)
                settled_wait(dve, "norms_taken", f)
                for t in range(TILES):
                    did(dve.max(top[:, t, :], norms[:, t, 0:ADAPTERS]))
                settle()
                did(dve.tensor_copy(wanted[:, :, 0:TOPK], top[:, :, 0:TOPK]))
                settled_wait(dve, "route_step", f, 3)
                for t in range(TILES):
                    did(dve.match_replace(replaced[:, t, :], wanted[:, t, :], norms[:, t, :], -2.0))
                settle()
                dve.tensor_scalar(chosen[:, :, :].rearrange("p t (q a) -> p t q a", q=4)[:, :, :, 0:RANK],
                                  replaced[:, :, 0:ADAPTERS].rearrange("p t (q a) -> p t q a", q=4),
                                  -1.5, None, ALU.is_lt).then_inc(S["routed"], 1)

            def choose(f, add):
                for v in range(4):
                    wait(dve, "spread_ready", f, v + 1)
                    if v == 0:
                        wait(dve, "vecs_ready", f)
                    part = vecs[:, 2 * v:2 * v + 2, :]
                    dve.tensor_tensor(part, part, spread[:, 2 * v:2 * v + 2, :], ALU.mult).then_inc(S["picked"], 1)
                if not add:
                    return
                wait(dve, "picked", f)
                dve.tensor_reduce(ssqT[:, :], vecs[:, :, :].rearrange("p j t -> p t j"), AX.X, ALU.add
                                  ).then_inc(S["vsum_ready"], 1)

            sums = scratch[:, 0, :]

            def inverse_sums(b, t):
                wait(dve, "pv_done", b, 2 * t + 1)
                if t:
                    wait(dve, "quotient_ready", b, t)
                dve.transpose(sums, bank("pv", 2 * t)[:, :]).then_inc(S["sums_taken"], 1)
                wait(dve, "sums_taken", b, t + 1)
                dve.reciprocal(inverse[:, :], sums.rearrange("p (k r) -> p k r", r=HD)[:, :, 0]
                               ).then_inc(S["norm_step"], 1)
                wait(dve, "norm_step", b, 2 * t + 1)
                dve.transpose(sums, inverse[:, :].unsqueeze(2).broadcast_to([P, DIM // HD, HD])
                              ).then_inc(S["norm_step"], 1)

            def quotient(b, t):
                wait(dve, "norm_step", b, 2 * t + 2)
                wait(dve, "pv_done", b, 2 * t + 2)
                if t:
                    wait(dve, "o_lo_ready", b, t)
                dve.tensor_tensor(scratch[:, 1, :], bank("pv", 2 * t + 1)[:, :], sums, ALU.mult
                                  ).then_inc(S["quotient_ready"], 1)

            def quotient_lo(b, t):
                wait(dve, "o_hi_ready", b, t + 1)
                dve.tensor_tensor(o_lo[:, t, :], scratch[:, 1, :], o_hi[:, t, :].bitcast(F32), ALU.subtract
                                  ).then_inc(S["o_lo_ready"], 1)

            def v_low(f):
                wait(dve, "v_hi_ready", f)
                dve.tensor_tensor(v_lo[:, :], bank("vsum", 0)[:, 0:SEQ], v_hi[:, :].bitcast(F32), ALU.subtract
                                  ).then_inc(S["v_lo_ready"], 1)

            def spread_v(f, b):
                if b is not None:
                    wait(dve, "pv_done", b)
                for k in range(2):
                    js = slice(4 * k, 4 * k + 4)
                    dve.tensor_tensor(u_hi[:, js, :], spread[:, js, :],
                                      v_hi[:, :].bitcast(F32).unsqueeze(1).broadcast_to([P, 4, SEQ]), ALU.mult
                                      ).then_inc(S["u_hi_ready"], 1)

            def low_queries(n, t):
                cols = slice(t * P, (t + 1) * P)
                wait(dve, "q_hi_ready", n, t + 1)
                dve.tensor_tensor(q_lo[:, :, cols].bitcast(F32R),
                                  bank("qkT", t)[:, :].rearrange("p (c q) -> p c q", c=CHUNKS),
                                  q_hi[:, :, cols], ALU.subtract).then_inc(S["q_lo_ready"], 1)

            def low_keys(n):
                wait(dve, "k_hi_ready", n)
                dve.tensor_tensor(k_lo.bitcast(F32R), bank("qkT", 2)[:, 0:SEQ], k_hi, ALU.subtract
                                  ).then_inc(S["k_lo_ready"], 1)

            def residual(b):
                did, settle = chain(dve, "y_step", b)
                for t in range(TILES):
                    wait(dve, "proj_done", b, t + 1)
                    if t == 0:
                        wait(dve, "res_loaded", b)
                    dve.scalar_tensor_tensor(out=x_res[:, t, :], in0=bank("proj", t)[:, :], scalar=gates[:, 0:1],
                                             in1=x_res[:, t, :], op0=ALU.mult, op1=ALU.add
                                             ).then_inc(S["x1_ready"], 1)
                    wait(dve, "x1_ready", b, t + 1)
                    did(dve.bn_stats(r_stats[:, t, :], x_res[:, t, :]))
                    settled_wait(dve, "y_step", b, 2 * t + 1)
                    did(dve.bn_aggr(r_aggr[:, t, :], r_stats[:, t, :]))
                    settle()
                    dve.tensor_scalar(r_rms[:, t:t + 1], r_aggr[:, t, 1:2], EPS, None, ALU.add
                                      ).then_inc(S["var_ready"], 1)
                    wait(dve, "y_rooted", b, t + 1)
                    dve.tensor_scalar(scratch[:, t, :], x_res[:, t, :], r_aggr[:, t, 0:1], r_rms[:, t:t + 1],
                                      ALU.subtract, ALU.mult).then_inc(S["y_ready"], 1)

            def result(f, t):
                wait(dve, "biased", f)
                wait(dve, "acc_done", f, t + 1)
                dve.scalar_tensor_tensor(out=x_out[:, t, :], in0=acc[t][:, :], scalar=gates[:, 1:2],
                                         in1=x_out[:, t, :], op0=ALU.mult, op1=ALU.add
                                         ).then_inc(S["out_ready"], 1)

            def step(i, here, before):
                f, n = i - 1, i + 1
                if here == "NX":
                    dve.memset(ones[:, :], 1.0).then_inc(S["fills"], 1)
                    dve.memset(k_stack[SHIFT_ROW:SHIFT_ROW + 1, :, :].bitcast(F32), 1.0).then_inc(S["fills"], 1)
                    dve.memset(norms[:, :, ADAPTERS:], -1.0).then_inc(S["fills"], 1)
                    dve.memset(wanted[:, :, :], -1.0).then_inc(S["fills"], 1)
                    dve.memset(chosen[:, :, :], 0.0).then_inc(S["fills"], 1)
                    dve.wait_ge(S["fills"], 5)
                    statistics(n)
                    tables(dve, "q_tables", HEADS, qw_b, q_cos, q_sin)
                    dve.wait_ge(S["q_tables"], 4 * TILES)
                    dve.wait_ge(S["const_loaded"], 16)
                    dve.tensor_copy(ident_bf[:, :], ident).then_inc(S["constants"], 1)
                if "A" in here:
                    maxima_of(i, range(0, 4))
                    if "N" in here and "F" in here:
                        rotate_queries(n, 0, 0, "A" in here)
                    maxima_of(i, range(4, 8))
                    if "N" in here and "F" in here:
                        rotate_queries(n, 0, 1, "A" in here)
                    maxima_of(i, range(8, HEADS))
                if here == "ANX":
                    statistics(n)
                    split_lo(dve, 5)
                    split_lo(dve, 6)
                if "N" in here:
                    if "F" not in here:
                        rotate_queries(n, 0, 0, "A" in here)
                        rotate_queries(n, 0, 1, "A" in here)
                    rotate_queries(n, 1, 0, "A" in here)
                    rotate_queries(n, 1, 1, "A" in here)
                    if here == "NX":
                        dve.wait_ge(S["k_tables"], 4 * TILES)
                    rotate_keys(n)
                if here == "ANX":
                    split_lo(dve, 7)
                if "F" in here:
                    route(f)
                    choose(f, "A" in here)
                if "A" in here:
                    inverse_sums(i, 0)
                    quotient(i, 0)
                if "N" in here and "F" not in here:
                    low_queries(n, 0)
                    low_queries(n, 1)
                    low_keys(n)
                if "N" in here and "F" in here:
                    low_keys(n)
                if "A" in here:
                    inverse_sums(i, 1)
                    quotient_lo(i, 0)
                    quotient(i, 1)
                if "N" in here and "F" in here:
                    low_queries(n, 0)
                    low_queries(n, 1)
                if "F" in here:
                    v_low(f)
                if "A" in here:
                    quotient_lo(i, 1)
                if "F" in here:
                    spread_v(f, i if "A" in here else None)
                if here == "NX":
                    dve.wait_ge(S["gated"], 1)
                    dve.tensor_scalar(gated_bias[:, :], gated_bias[:, :], gates[:, 1:2], None, ALU.mult
                                      ).then_inc(S["gated"], 1)
                    split_lo(dve, 2)
                    split_lo(dve, 3)
                if "A" in here:
                    residual(i)
                if "F" in here and "X" in here:
                    statistics(n + 1)
                if "F" in here:
                    result(f, 0)
                if "A" in here:
                    for t in range(TILES):
                        wait(dve, "yT_hi_ready", i, t + 1)
                        cols = slice(t * P, (t + 1) * P)
                        dve.tensor_tensor(yT_lo[:, :, cols],
                                          bank("yT", t)[:, :].rearrange("p (c q) -> p c q", c=CHUNKS),
                                          yT_hi[:, :, cols].bitcast(F32), ALU.subtract
                                          ).then_inc(S["yT_lo_ready"], 1)
                if "F" in here:
                    result(f, 1)
                if here == "ANX":
                    statistics(n + 1)

            run(dve, step)

        @block.gpsimd
        def _(pool):
            def step(i, here, before):
                f, n = i - 1, i + 1

                def root(batch):
                    wait(pool, "rms_ready", batch)
                    flat = rms[:, :, :].rearrange("p a t -> p (a t)")
                    pool.tensor_tensor(flat, flat, minus_half[:, :], ALU.pow).then_inc(S["rooted"], 1)

                if here == "NX":
                    pool.memset(minus_half[:, :], -0.5).then_inc(S["exponents"], 1)
                    pool.wait_ge(S["exponents"], 1)
                    root(0)
                    tables(pool, "k_tables", KV, kw_b, k_cos, k_sin)
                    split_lo(pool, 0)
                    split_lo(pool, 1)
                    wait(pool, "k_lo_ready", 0)
                    for g in range(KV):
                        stack_keys(pool, g, f"first_keys{g}")
                    split_lo(pool, 4)
                    root(1)
                if "F" in here:
                    wait(pool, "x1_ready", f)
                    wait(pool, "x_out_free", f)
                    pool.wait_ge(S["gated"], 2)
                    pool.tensor_tensor(x_out[:, :, :], x_res[:, :, :],
                                       gated_bias[:, :].unsqueeze(1).broadcast_to([P, TILES, DIM]), ALU.add
                                       ).then_inc(S["biased"], 1)
                if "A" in here:
                    for u in range(8):
                        t, g = u // KV, u % KV
                        block_ = (probs1[:, g, 1, :] if t else probs0[:, g, :]).rearrange("p (n q) -> p n q", n=GROUP)
                        settled_wait(pool, "exp_done", i, 5 + 2 * g if t else g + 1)
                        pool.affine_select(out=block_, in_=block_, compare_op=ALU.is_ge, fill=0.0, base=0,
                                           pattern=[[0, GROUP], [1, P]], channel_multiplier=-1
                                           ).then_inc(S["masked"], 1)
                if here == "ANX":
                    for c in range(len(stage), len(W_PIECES)):
                        split_lo(pool, c)
                if "F" in here:
                    wait(pool, "v_lo_ready", f)
                    if "A" in here:
                        wait(pool, "pv_done", i)
                    for k in range(2):
                        js = slice(4 * k, 4 * k + 4)
                        pool.tensor_tensor(u_lo[:, js, :], spread[:, js, :],
                                           v_lo[:, :].bitcast(F32).unsqueeze(1).broadcast_to([P, 4, SEQ]), ALU.mult
                                           ).then_inc(S["u_lo_ready"], 1)
                if "A" in here:
                    for t in range(TILES):
                        wait(pool, "var_ready", i, t + 1)
                        pool.tensor_tensor(r_rms[:, t:t + 1], r_rms[:, t:t + 1], minus_half[:, 0:1], ALU.pow
                                           ).then_inc(S["y_rooted"], 1)
                if "X" in here and here != "NX":
                    root(n + 1)

            run(pool, step)


W_PIECES = [("o", 0), ("o", 1), ("a", 0), ("a", 1), ("a", 2), ("a", 3), ("w", 0), ("w", 1),
            ("b", 0), ("b", 1), ("b", 2), ("b", 3)]
PIECE = 1024
LO_BY_POOL, LO_BY_DVE, X_OUT_LAST = (0, 1, 4, 9, 10, 11), (2, 3, 5, 6, 7), 8


def w_part(w, c):
    name, k = W_PIECES[c]
    return w[name][:, :, :].rearrange("p a b -> p (a b)")[:, k * PIECE:(k + 1) * PIECE]


def constants():
    t = np.zeros((P, N_CONST), np.float32)

    def put(name, value):
        t[:, slice(*CONST_COLS[name])] = np.asarray(value, np.float32).reshape(P, -1)

    r = np.arange(P)
    put("ident", np.eye(P))
    put("spread_sum", (r[:, None] % RANK == r[None, :] % RANK) / TOPK ** 2)
    col = np.arange(HD)
    put("pick", np.stack([col[None, :] == parity * PER_CHUNK + r[:, None] // RANK for parity in range(2)], 1))
    k = np.arange(P)
    diagonal = np.where(k[None, :] <= r[:, None], 0.0, NEG)
    put("mask", np.concatenate([np.zeros((P, P)), diagonal], 1))
    inv = (np.float32(1.0) / np.float32(10000.0) ** (np.arange(0, HD, 2, dtype=np.float32) / np.float32(HD)))
    freqs = np.outer(np.arange(SEQ, dtype=np.float32), inv.astype(np.float32)).astype(np.float32)
    cos = np.concatenate([np.cos(freqs), np.cos(freqs)], 1)
    sin = np.concatenate([-np.sin(freqs), np.sin(freqs)], 1)
    put("cos", cos.reshape(TILES, P, HD).transpose(1, 0, 2))
    put("sin", sin.reshape(TILES, P, HD).transpose(1, 0, 2))
    j = np.arange(ROUTES)
    row = HD * (j // 2) + (j % 2) * PER_CHUNK
    put("expand", r[:, None, None] == row[None, :, None] + r[None, None, :] // RANK)
    return t


def kernel(**inputs):
    import concourse.bacc as bacc
    from concourse.bass_utils import run_bass_kernel_spmd

    w_out, A, B, W = (np.asarray(inputs[k]) for k in ("L0_xattn_w_out", "L0_ffn_A", "L0_ffn_B", "L0_ffn_W"))
    o = w_out.reshape(DIM, KV, GROUP, HD).transpose(1, 3, 2, 0).reshape(P, CHUNKS * DIM)
    at = A.reshape(ADAPTERS * RANK, CHUNKS, P).transpose(2, 1, 0).reshape(P, -1)
    wt = W.reshape(DIM, CHUNKS, P).transpose(2, 1, 0).reshape(P, -1)
    bt = B.transpose(0, 2, 1).reshape(ROUTES, P, DIM).transpose(1, 0, 2).reshape(P, -1)
    pieces = np.concatenate([o, at, wt, bt], 1).reshape(P, len(W_PIECES), PIECE).transpose(1, 0, 2)
    given = {
        "x": inputs["x"], "ctx": inputs["ctx_512"], "weights": pieces, "const": constants(),
        "qw": np.asarray(inputs["L0_xattn_q_norm_w"]).reshape(1, DIM),
        "kw": np.asarray(inputs["L0_xattn_k_norm_w"]).reshape(1, CTX),
        "bias": np.asarray(inputs["L0_ffn_bias"]).reshape(1, DIM),
        "g_x": np.asarray(inputs["g_xattn"]).reshape(1, 1), "g_f": np.asarray(inputs["g_ffn"]).reshape(1, 1),
    }
    nc = bacc.Bacc("TRN2", target_bir_lowering=False, num_devices=1)
    arrays, a = {}, {}
    for name, value in given.items():
        value = np.ascontiguousarray(value)
        arrays[f"in_{name}"] = value
        a[name] = nc.dram_tensor(f"in_{name}", value.shape, mybir.dt.from_np(value.dtype), kind="ExternalInput").ap()
    a["out"] = nc.dram_tensor("out_0", (BATCHES, SEQ, DIM), F32, kind="ExternalOutput").ap()
    build(nc, a)
    r = run_bass_kernel_spmd(nc, [arrays], core_ids=[0])
    return r.results[0]["out_0"]
```
